# Optimizing a Trainium2 kernel written in Bass

```python
import numpy as np
import jax
import jax.numpy as jnp

def _softmax(x, axis=-1):
    return jax.nn.softmax(x, axis=axis)

def _gelu(x):
    return jax.nn.gelu(x, approximate=True)

def _silu(x):
    return jax.nn.silu(x)

def _sigmoid(x):
    return jax.nn.sigmoid(x)

def _layernorm(x, axis=-1, eps=1e-05):
    m = jnp.mean(x, axis=axis, keepdims=True)
    v = jnp.var(x, axis=axis, keepdims=True)
    return (x - m) / jnp.sqrt(v + eps)

def _scatter_add(tgt, idx, src, axis=0):
    return tgt.at[idx].add(src)

def _segment_sum(src, seg, n):
    return jax.ops.segment_sum(src, seg, n)
kernel_name = 'mk_flamingo_gated_d1_seqx_r4_f5b802'

def setup_inputs(seed: int=0):
    np.random.seed(seed)
    _w = jnp.asarray

    def _rec_inputs():
        import jax
        import jax.numpy as jnp
        _rk = jax.random.key(seed)
        x = 0.5 + 0.2887 * jax.random.normal(jax.random.fold_in(_rk, 1), (4, 512, 512), jnp.float32)
        _lenS = 512 - jax.random.randint(jax.random.fold_in(_rk, 7), (4,), 0, max(1, 512 // 4) + 1, jnp.int32)
        _lenS2 = 512 - jax.random.randint(jax.random.fold_in(_rk, 8), (4,), 0, max(1, 512 // 4) + 1, jnp.int32)
        _ctx_512P = jax.random.normal(jax.random.fold_in(_rk, 11), (4, 16, 128), jnp.float32)
        _ctx_512c = jax.random.dirichlet(jax.random.fold_in(_rk, 511), 0.3 * jnp.ones((16,), jnp.float32), (4, 512))
        _ctx_512t = jnp.einsum('bsk,bkd->bsd', _ctx_512c, _ctx_512P)
        _ctx_512t = _ctx_512t * jax.lax.rsqrt(jnp.mean(jnp.square(_ctx_512t)) + 1e-12) * 0.953939
        ctx_512 = -0.000392918 + 0.999932 * (_ctx_512t + 0.3 * jax.random.normal(jax.random.fold_in(_rk, 611), (4, 512, 128), jnp.float32))
        _g = jax.random.normal(jax.random.fold_in(_rk, 9001), (2, 1), jnp.float32)
        _g = jnp.sign(_g) * jnp.maximum(jnp.abs(_g), 1.0) + (_g == 0) * 1.0
        g_xattn = _g[0]
        g_ffn = _g[1]
        return (x, ctx_512, g_xattn, g_ffn)
    x, ctx_512, g_xattn, g_ffn = _rec_inputs()

    def _L0_xattn_setup():
        import jax, jax.numpy as jnp
        import numpy as np
        B, N, D = (16, 512, 128)
        H = 4
        TOP_K_RATIO = 0.3
        key = jax.random.key(seed)
        k1, k2, k3, k4 = jax.random.split(key, 4)
        h = jax.random.normal(k1, (B, N, D), dtype=jnp.float32)
        adj_raw = jax.random.uniform(k2, (B, N, N), dtype=jnp.float32)
        lim = 1.0 / np.sqrt(D)
        Wq = jax.random.uniform(k3, (D, D), minval=-lim, maxval=lim, dtype=jnp.float32)
        Wk = jax.random.uniform(k4, (D, D), minval=-lim, maxval=lim, dtype=jnp.float32)
        gamma_raw = jnp.float32(-0.85)
        return {'h': h, 'adj_raw': adj_raw, 'Wq': Wq, 'Wk': Wk, 'gamma_raw': gamma_raw}
    _L0_xattn_all = _L0_xattn_setup()
    _L0_xattn_in = {k: v for k, v in _L0_xattn_all.items() if k in ('Wq', 'Wk', 'gamma_raw')}
    del _L0_xattn_all

    def _L0_ffn_setup():
        import jax, jax.numpy as jnp
        import numpy as np
        NUM_ACT = 2
        key = jax.random.key(seed)
        k1, k2, k3, k4, k5 = jax.random.split(key, 5)
        B, S, D, I, E = (4, 128, 512, 1024, 8)
        x = jax.random.normal(k1, (B, S, D), dtype=jnp.float32)
        gate_w = jax.random.normal(k2, (E, D), dtype=jnp.float32) * 0.02
        w1 = jax.random.normal(k3, (E, I, D), dtype=jnp.float32) * 0.02
        w2 = jax.random.normal(k4, (E, D, I), dtype=jnp.float32) * 0.02
        w3 = jax.random.normal(k5, (E, I, D), dtype=jnp.float32) * 0.02
        return {'x': x, 'gate_w': gate_w, 'w1': w1, 'w2': w2, 'w3': w3}
    _L0_ffn_all = _L0_ffn_setup()
    _L0_ffn_in = {k: v for k, v in _L0_ffn_all.items() if k in ('gate_w', 'w1', 'w2', 'w3')}
    del _L0_ffn_all
    return {'x': x, 'ctx_512': ctx_512, 'g_xattn': g_xattn, 'g_ffn': g_ffn, 'L0_xattn_Wq': _L0_xattn_in['Wq'], 'L0_xattn_Wk': _L0_xattn_in['Wk'], 'L0_xattn_gamma_raw': _L0_xattn_in['gamma_raw'], 'L0_ffn_gate_w': _L0_ffn_in['gate_w'], 'L0_ffn_w1': _L0_ffn_in['w1'], 'L0_ffn_w2': _L0_ffn_in['w2'], 'L0_ffn_w3': _L0_ffn_in['w3']}

def reference(x, ctx_512, g_xattn, g_ffn, L0_xattn_Wq, L0_xattn_Wk, L0_xattn_gamma_raw, L0_ffn_gate_w, L0_ffn_w1, L0_ffn_w2, L0_ffn_w3):
    import jax
    import jax.numpy as jnp

    def _L0_xattn_ref(h, adj_raw, Wq, Wk, gamma_raw):
        import jax, jax.numpy as jnp
        import numpy as np
        B, N, D = (16, 512, 128)
        H = 4
        TOP_K_RATIO = 0.3
        b, n, dm = h.shape
        d = dm // H
        Q = (h @ Wq.T).reshape(b, n, H, d).transpose(0, 2, 1, 3)
        K = (h @ Wk.T).reshape(b, n, H, d).transpose(0, 2, 1, 3)
        sim = jnp.einsum('bhnd,bhmd->bnm', Q, K) / (jnp.sqrt(jnp.float32(d)) * H)
        k = max(1, int(n * TOP_K_RATIO))
        topk_vals = jax.lax.top_k(sim, k)[0]
        threshold = topk_vals[:, :, -1:]
        sparse_mask = (sim >= threshold).astype(sim.dtype)
        A_learned = jax.nn.sigmoid(sim) * sparse_mask
        A_learned = (A_learned + jnp.swapaxes(A_learned, -1, -2)) * 0.5
        gamma = jax.nn.sigmoid(gamma_raw)
        return (1.0 - gamma) * adj_raw + gamma * A_learned

    def _L0_ffn_ref(x, gate_w, w1, w2, w3):
        import jax, jax.numpy as jnp
        import numpy as np
        NUM_ACT = 2
        B, S, D = x.shape
        xt = x.reshape(-1, D)
        scores = jnp.einsum('ti,ei->te', xt, gate_w)
        probs = jax.nn.softmax(scores, axis=-1)
        expert_weights, expert_indices = jax.lax.top_k(probs, NUM_ACT)
        expert_weights = expert_weights / expert_weights.sum(axis=-1, keepdims=True)
        x1 = jax.nn.silu(jnp.einsum('ti,eoi->teo', xt, w1))
        x3 = jnp.einsum('ti,eoi->teo', xt, w3)
        expert_outs_all = jnp.einsum('teo,eio->tei', x1 * x3, w2)
        sel = jnp.take_along_axis(expert_outs_all, expert_indices[:, :, None], axis=1)
        out = jnp.einsum('tai,ta->ti', sel, expert_weights)
        return out.reshape(B, S, D)
    x = x + jnp.tanh(g_xattn[0]) * _L0_xattn_ref(ctx_512, _layernorm(x, axis=-1), L0_xattn_Wq, L0_xattn_Wk, L0_xattn_gamma_raw)
    x = x + jnp.tanh(g_ffn[0]) * _L0_ffn_ref(_layernorm(x, axis=-1), L0_ffn_gate_w, L0_ffn_w1, L0_ffn_w2, L0_ffn_w3)
    return x

_drawn_inputs = setup_inputs


def setup_inputs(seed=0):
    import zlib

    import numpy as np

    out = dict(_drawn_inputs(seed))
    spreads = {}
    factors = {}
    for name, (base, spread) in spreads.items():
        noise = np.random.default_rng([zlib.crc32(name.encode()), seed]).standard_normal(out[name].shape)
        drawn = base * np.exp(spread * noise) if base else spread * noise
        out[name] = jnp.asarray(drawn.astype(out[name].dtype))
    for name, factor in factors.items():
        out[name] = (out[name] * factor).astype(out[name].dtype)
    return out
```

```python
from contextlib import ExitStack

import concourse.bass as bass
from concourse import mybir

F32 = mybir.dt.float32
F32R = mybir.dt.float32r
BF16 = mybir.dt.bfloat16
I8 = mybir.dt.int8
I32 = mybir.dt.int32
U32 = mybir.dt.uint32
ALU = mybir.AluOpType
ACT = mybir.ActivationFunctionType
AX = mybir.AxisListType

P = 128
B, N, D = 4, 512, 512
TOKENS = B * N
TB = N // P
TILES = B * TB
HALF = TILES // 2
KTH = int(N * 0.3)
SIM_SCALE = 1.0 / (32.0 ** 0.5 * 4.0)
EPS = 1e-5
E, I = 8, 1024
DC = D // P
IC = I // P
COLS = 512
REGION = TOKENS + P
META = D
ROW = D + E + 1
GROUPS, OPS, OPW = 3, 4, 1024
SEARCH = 4
ON_VECTOR = 3
WINDOW = 8
AIM = KTH - (WINDOW + 1) / 2
BIG = 3.0e38
MOST_BLOCKS = 2 * TOKENS // P + E


def build(nc, x, ctxT, wqT, wkT, gateT, weights, gains, out):
    routed = nc.dram_tensor("routed", (E * REGION, ROW), F32).ap()
    x_tiles = x.rearrange("(b i p) d -> b p i d", p=P, i=TB)
    out_tiles = out[0:TOKENS, :].rearrange("(b i p) d -> b p i d", p=P, i=TB)
    w_groups = weights.rearrange("e p (q n) -> e q p n", q=GROUPS)

    stack = ExitStack()
    with stack:
        def sb(name, shape, dt=F32, on=stack):
            return on.enter_context(nc.sbuf_tensor(name, shape, dt))

        def sem(name):
            return stack.enter_context(nc.semaphore(name))

        raw = sb("raw", [P, GROUPS, OPS * OPW])
        w_hi = [sb(f"w{q}_hi", [P, OPS, OPW], F32R) for q in range(2)]
        w_lo = [sb(f"w{q}_lo", [P, OPS, OPW], F32R) for q in range(2)]
        ident = sb("ident", [P, P])
        meta_next = sb("meta_next", [P, E])
        meta_now = sb("meta_now", [P, E])
        token_next = sb("token_next", [P, 1], I32)
        token_now = sb("token_now", [P, 1], I32)
        token_out = sb("token_out", [P, 1], I32)
        y_row = sb("y_row", [P, 1], I32)
        no_shift = sb("no_shift", [P, 1], I32)
        told = sb("told", [P, 1], I32)
        table = sb("table", [1, 4 * E], I32)
        pad = sb("pad", [P, ROW])
        pad_at = sb("pad_at", [P, E], I32)

        part1 = ExitStack()
        S = sb("S", [P, TILES, N], F32, part1)
        work = sb("work", [P, 7168], F32, part1)
        xb = sb("xb", [P, 2, TB, D], F32, part1)
        rows = sb("rows", [P, TB, ROW], F32, part1)
        wq = sb("wq", [P, P], F32, part1)
        wk = sb("wk", [P, P], F32, part1)
        gate_w = sb("gate_w", [P, DC, E], F32, part1)
        upper = sb("upper", [P, P], BF16, part1)
        ones_b = sb("ones_b", [P, P], BF16, part1)
        ones_f = sb("ones_f", [P, P], F32, part1)
        gain_in = sb("gain_in", [P, 3], F32, part1)
        gain = sb("gain", [P, 6], F32, part1)
        tanh_x, gamma, tanh_f, c1, c2, neg_c1 = (gain[:, k:k + 1] for k in range(6))
        small = sb("small", [P, 16], F32, part1)
        sim_stats = sb("sim_stats", [P, B, TB, 6], F32, part1)
        sim_mv = sb("sim_mv", [P, TILES, 2], F32, part1)
        sim_sd = sb("sim_sd", [P, TILES], F32, part1)
        half_pow = sb("half_pow", [P, TILES], F32, part1)
        rsqrt_pow = sb("rsqrt_pow", [P, TB], F32, part1)
        low = sb("low", [P, TILES, 2], F32, part1)
        high = sb("high", [P, TILES, 2], F32, part1)
        probe = sb("probe", [P, TILES, 2], F32, part1)
        act_sum = sb("act_sum", [P, TILES], F32, part1)
        is_low = sb("is_low", [P, HALF, 2], I32, part1)
        is_high = sb("is_high", [P, HALF, 2], I32, part1)
        in_window = sb("in_window", [P, TILES], I32, part1)
        span = sb("span", [P, HALF, 2], F32, part1)
        frac = sb("frac", [P, HALF], F32, part1)
        inv = sb("inv", [P, HALF], F32, part1)
        count = sb("count", [P, TILES], F32, part1)
        top8 = sb("top8", [P, TILES, 8], F32, part1)
        rank8 = sb("rank8", [P, TILES, 8], F32, part1)
        pick = sb("pick", [P, TILES, 8], F32, part1)
        thr = sb("thr", [P, TILES], F32, part1)
        settled = sb("settled", [P, 1], F32, part1)
        settled_i = sb("settled_i", [P, 1], I32, part1)
        max8 = sb("max8", [P, 8], F32, part1)
        ln_stats = sb("ln_stats", [P, TB, 6], F32, part1)
        ln_mv = sb("ln_mv", [P, 2, TB, 2], F32, part1)
        ln_r = sb("ln_r", [P, 2, TB], F32, part1)
        ln_s = sb("ln_s", [P, 2, TB], F32, part1)
        ln_o = sb("ln_o", [P, 2, TB], F32, part1)
        score = sb("score", [P, TB, E], F32, part1)
        best = sb("best", [P, TB, 8], F32, part1)
        best_at = sb("best_at", [P, TB, 8], U32, part1)
        best_f = sb("best_f", [P, TB, 2], F32, part1)
        lead = sb("lead", [P, TB, 2], F32, part1)
        share = sb("share", [P, TB, 2], F32, part1)
        expert_no = sb("expert_no", [P, TB, 2, E], F32, part1)
        chosen = sb("chosen", [P, TB, 2, E], F32, part1)
        weighed = sb("weighed", [P, TB, 2, E], F32, part1)
        mask = sb("mask", [P, TB, E], BF16, part1)
        before = sb("before", [P, B + 1, E], BF16, part1)
        mask_sum = sb("mask_sum", [P, E], F32, part1)
        region_row = sb("region_row", [P, TB, E], F32, part1)
        pad_row = sb("pad_row", [P, E], F32, part1)
        place = sb("place", [P, TB, E], F32, part1)
        place_of = sb("place_of", [P, TB, 2, E], F32, part1)
        place_f = sb("place_f", [P, TB, 2], F32, part1)
        place_i = sb("place_i", [P, TB, 2], I32, part1)
        token_no = sb("token_no", [P, TILES], I32, part1)
        pad_f = sb("pad_f", [P, E], F32, part1)
        blk_i = sb("blk_i", [P, E], I32, part1)
        blk_j = sb("blk_j", [P, E], I32, part1)
        blk_f = sb("blk_f", [P, E], F32, part1)
        blk_1 = sb("blk_1", [P, E], F32, part1)
        table_f = sb("table_f", [P, 4 * E], F32, part1)
        part1.close()

        xtile = sb("xtile", [P, ROW])
        xT_hi = sb("xT_hi", [P, DC, P], F32R)
        xT_lo = sb("xT_lo", [P, DC, P], F32R)
        hT_hi = sb("hT_hi", [P, 2, COLS], F32R)
        hT_lo = sb("hT_lo", [P, 2, COLS], F32R)
        act_g = sb("act_g", [P, 2, COLS])
        h = sb("h", [P, 2, COLS])
        y = sb("y", [P, D])
        w_hi.append(sb("w2_hi", [P, OPS, OPW], F32R))
        w_lo.append(sb("w2_lo", [P, OPS, OPW], F32R))

        ctx_sb = work[:, 0:2048].rearrange("p (b n) -> p b n", b=B)
        QT, KT = work[:, 2048:2560], work[:, 2560:3072]
        flags = [work[:, 3072 + 256 * k:3328 + 256 * k].bitcast(BF16) for k in range(ON_VECTOR)]
        signs = [work[:, 3840 + 128 * k:3968 + 128 * k].bitcast(I8) for k in range(2 * (HALF - ON_VECTOR))]
        masked = [work[:, 5120 + 512 * k:5632 + 512 * k] for k in range(2)]
        left_over = masked[0]
        A = [work[:, 2048 * k:2048 * (k + 1)].rearrange("p (i n) -> p i n", i=TB) for k in range(2)]
        xfT = [work[:, 6144 + 512 * k:6656 + 512 * k] for k in range(2)]

        bank = [stack.enter_context(nc.psum_tensor(f"bank{k}", [P, COLS], F32)) for k in range(8)]
        GATE, UP, Y_BANK, X_BANK = (0, 2), (1, 3), 7, 6
        H_BANK = (4, 5)
        scores_ps = bank[6][:, 0:TB * E].rearrange("p (i e) -> p i e", e=E)
        rank_ps = bank[7][:, 0:TB * E].rearrange("p (i e) -> p i e", e=E)
        total_ps = bank[0][:, 0:E]
        settled_ps = bank[6][:, 64:65]

        wqk_in, ctx_in, gate_in, gain_in_s = sem("wqk_in"), sem("ctx_in"), sem("gate_in"), sem("gain_in_s")
        x_in = [sem("x_in0"), sem("x_in1")]
        raw_in = [sem(f"raw_in{q}") for q in range(GROUPS)]
        raw_in_0 = [sem(f"raw_in_0_{q}") for q in range(GROUPS)]
        consts = sem("consts")
        qk_mm, qk_out, sim_mm, sim_out = sem("qk_mm"), sem("qk_out"), sem("sim_mm"), sem("sim_out")
        sim_moments, sd_set = sem("sim_moments"), sem("sd_set")
        probe_set = [sem("probe_set0"), sem("probe_set1")]
        act_counted = [sem("act_counted0"), sem("act_counted1")]
        settled_set, settled_mm, thr_set = sem("settled_set"), sem("settled_mm"), sem("thr_set")
        gains_act, gains_set = sem("gains_act"), sem("gains_set")
        ln1_stats, ln2_stats, base_set = sem("ln1_stats"), sem("ln2_stats"), sem("base_set")
        sig_set, A_set, AA_mm, x1_set = sem("sig_set"), sem("A_set"), sem("AA_mm"), sem("x1_set")
        x1_stored = [sem("x1_stored0"), sem("x1_stored1")]
        trash_stored = sem("trash_stored")
        rows_set, xfT_mm, xfT_out, scores_mm = sem("rows_set"), sem("xfT_mm"), sem("xfT_out"), sem("scores_mm")
        lead_set, share_set, mask_set, rank_mm = sem("lead_set"), sem("share_set"), sem("mask_set"), sem("rank_mm")
        place_set, routed_in, total_mm = sem("place_set"), sem("routed_in"), sem("total_mm")
        pad_set, table_set = sem("pad_set"), sem("table_set")
        hi_set = [sem(f"hi_set{q}") for q in range(GROUPS)]
        lo_set = [sem(f"lo_set{q}") for q in range(GROUPS)]
        xtile_free, y_out, y_free = sem("xtile_free"), sem("y_out"), sem("y_free")
        xtile_in, xT_mm, xhi_set, xT_set = sem("xtile_in"), sem("xT_mm"), sem("xhi_set"), sem("xT_set")
        gate_mm, up_mm = [sem("gate_mm0"), sem("gate_mm1")], [sem("up_mm0"), sem("up_mm1")]
        silu_set, h_set = [sem("silu_set0"), sem("silu_set1")], [sem("h_set0"), sem("h_set1")]
        hT_mm, hhi_set = [sem("hT_mm0"), sem("hT_mm1")], [sem("hhi_set0"), sem("hhi_set1")]
        hT_set = [sem("hT_set0"), sem("hT_set1")]
        y_mm, y_set, y_added = sem("y_mm"), sem("y_set"), sem("y_added")

        def entry(eng, row, e, least, most):
            return eng.value_load(table[0:1, bass.ds(e + row * E, 1)], min_val=least, max_val=most)

        def blocks(eng, e):
            first = entry(eng, 0, e, 0, MOST_BLOCKS - 1)
            end = entry(eng, 1, e, 1, MOST_BLOCKS)
            return eng.Fori(first, end)

        block = stack.enter_context(nc.Block())

        @block.sync
        def _(sp):
            sp.dma_start(wq[:, :], wqT).then_inc(wqk_in, 16)
            sp.dma_start(wk[:, :], wkT).then_inc(wqk_in, 16)
            sp.dma_start(ctx_sb, ctxT).then_inc(ctx_in, 16)
            sp.dma_start(gain_in[:, :], gains.partition_broadcast(P)).then_inc(gain_in_s, 16)
            sp.dma_start(gate_w[:, :, :], gateT).then_inc(gate_in, 16)
            for b in range(2):
                sp.dma_start(xb[:, b, :, :], x_tiles[b]).then_inc(x_in[b], 16)
            for q in range(GROUPS):
                sp.dma_start(raw[:, q, :], w_groups[0, q]).then_inc(raw_in_0[q], 16)
            for b in range(B):
                sp.wait_ge(x1_set, TB * (b + 1))
                sp.dma_start(out_tiles[b], xb[:, b % 2, :, :]).then_inc(x1_stored[b % 2], 16)
                if b + 2 < B:
                    sp.wait_ge(x1_stored[b % 2], 16 * (b // 2 + 1))
                    sp.wait_ge(rows_set, b + 1)
                    sp.dma_start(xb[:, b % 2, :, :], x_tiles[b + 2]).then_inc(x_in[b % 2], 16)
            sp.wait_ge(table_set, 1)
            sp.wait_ge(routed_in, 16 * (2 * TILES + E))
            with sp.Fori(0, E) as e:
                first = entry(sp, 0, e, 0, MOST_BLOCKS - 1)
                some = entry(sp, 3, e, 1, REGION // P)
                with sp.Fori(0, some) as j:
                    sp.wait_ge(xtile_free, first + j + 1)
                    sp.dma_start(xtile[:, :], routed[bass.ds(e * REGION + j * P, P), :]).then_inc(xtile_in, 16)
            end = sp.value_load(table[0:1, 2 * E - 1:2 * E], min_val=1, max_val=MOST_BLOCKS)
            sp.wait_ge(xtile_free, end + 1)
            sp.dma_start(xtile[:, :], routed[0:P, :]).then_inc(xtile_in, 16)

        @block.gpsimd
        def _(pool):
            nc.gpsimd.memset(half_pow[:, :], 0.5)
            nc.gpsimd.memset(rsqrt_pow[:, :], -0.5)
            nc.gpsimd.memset(ident[:, :], 0.0)
            nc.gpsimd.memset(no_shift[:, :], 0)
            nc.gpsimd.memset(upper[:, :], 1.0)
            nc.gpsimd.memset(ones_b[:, :], 1.0)
            nc.gpsimd.memset(ones_f[:, :], 1.0)
            nc.gpsimd.memset(pad[:, :], 0.0)
            nc.gpsimd.memset(before[:, 0, :], 0.0)
            nc.gpsimd.iota(rank8[:, :, :], [[0, TILES], [1, 8]], 1, 0, allow_small_or_imprecise_dtypes=True)
            nc.gpsimd.iota(expert_no[:, :, :, :], [[0, 2 * TB], [1, E]], 0, 0, allow_small_or_imprecise_dtypes=True)
            nc.gpsimd.iota(region_row[:, :, :], [[0, TB], [REGION, E]], 0, 0, allow_small_or_imprecise_dtypes=True)
            nc.gpsimd.iota(pad_row[:, :], [[REGION, E]], 0, 1, allow_small_or_imprecise_dtypes=True)
            nc.gpsimd.iota(token_no[:, :], [[P, TILES]], 0, 1)
            pool.drain()
            nc.gpsimd.affine_select(out=ident[:, :], in_=ident[:, :], compare_op=ALU.not_equal, fill=1.0,
                                    base=0, pattern=[[-1, P]], channel_multiplier=1)
            nc.gpsimd.affine_select(out=upper[:, :], in_=upper[:, :], compare_op=ALU.is_gt, fill=0.0,
                                    base=0, pattern=[[1, P]], channel_multiplier=-1)
            nc.gpsimd.iota(pad[:, ROW - 1:ROW].bitcast(I32), [[0, 1]], TOKENS, 1)
            pool.drain()
            nc.gpsimd.memset(small[:, 0:1], 0.0).then_inc(consts, 1)
            pool.wait_ge(consts, 1)
            pool.dma_start(out[TOKENS:TOKENS + P, :], pad[:, 0:D]).then_inc(trash_stored, 16)

            pool.wait_ge(sim_moments, 1)
            nc.gpsimd.tensor_tensor(sim_sd[:, :], sim_mv[:, :, 1], half_pow[:, :], ALU.pow).then_inc(sd_set, 1)

            def scales(k, stats, n):
                pool.wait_ge(stats, n)
                nc.gpsimd.tensor_scalar(ln_s[:, k, :], ln_mv[:, k, :, 1], EPS, 1.0, ALU.add, ALU.mult)
                pool.drain()
                nc.gpsimd.tensor_tensor(ln_r[:, k, :], ln_s[:, k, :], rsqrt_pow[:, :], ALU.pow)
                pool.drain()
                nc.gpsimd.tensor_tensor(ln_o[:, k, :], ln_r[:, k, :], ln_mv[:, k, :, 0], ALU.mult)

            def base(b):
                pool.wait_ge(x_in[b % 2], 16 * (b // 2 + 1))
                scales(0, ln1_stats, b + 1)
                if b == 0:
                    pool.wait_ge(gains_set, 1)
                nc.gpsimd.tensor_scalar(ln_s[:, 0, :], ln_r[:, 0, :], c1, 1.0, ALU.mult, ALU.add)
                pool.drain()
                nc.gpsimd.tensor_scalar(ln_o[:, 0, :], ln_o[:, 0, :], neg_c1, 1.0, ALU.mult, ALU.mult)
                pool.drain()
                for i in range(TB):
                    nc.gpsimd.tensor_scalar(xb[:, b % 2, i, :], xb[:, b % 2, i, :], ln_s[:, 0, i:i + 1],
                                            ln_o[:, 0, i:i + 1], ALU.mult, ALU.add).then_inc(base_set, 1)

            def normal_rows(b):
                scales(1, ln2_stats, b + 1)
                pool.drain()
                nc.gpsimd.tensor_scalar(ln_o[:, 1, :], ln_o[:, 1, :], -1.0, 1.0, ALU.mult, ALU.mult)
                pool.drain()
                if b > 0:
                    pool.wait_ge(routed_in, 16 * 2 * TB * b)
                for i in range(TB):
                    last = nc.gpsimd.tensor_scalar(rows[:, i, 0:D], xb[:, b % 2, i, :], ln_r[:, 1, i:i + 1],
                                                   ln_o[:, 1, i:i + 1], ALU.mult, ALU.add)
                last.then_inc(rows_set, 1)

            def route(b):
                pool.wait_ge(place_set, b + 1)
                for i in range(TB):
                    for k in range(2):
                        nc.gpsimd.indirect_dma_start(
                            routed, bass.IndirectOffsetOnAxis(ap=place_i[:, i, k:k + 1], axis=0),
                            rows[:, i, :], None, bounds_check=E * REGION - 1, oob_is_err=True,
                        ).then_inc(routed_in, 16)

            base(0)
            for b in range(B):
                if b + 1 < B:
                    base(b + 1)
                normal_rows(b)
                route(b)
            pool.wait_ge(pad_set, 1)
            for e in range(E):
                nc.gpsimd.indirect_dma_start(
                    routed, bass.IndirectOffsetOnAxis(ap=pad_at[:, e:e + 1], axis=0),
                    pad[:, :], None, bounds_check=E * REGION - 1, oob_is_err=True,
                ).then_inc(routed_in, 16)

            pool.wait_ge(table_set, 1)
            pool.wait_ge(trash_stored, 16)
            for k in range(2):
                pool.wait_ge(x1_stored[k], 16 * (B // 2))
            nc.gpsimd.tensor_tensor(told[:, :], no_shift[:, :], no_shift[:, :], ALU.add).then_inc(y_free, 1)
            pool.drain()

            def add_blocks(e):
                with blocks(pool, e) as g:
                    pool.wait_ge(y_set, g + 1)
                    nc.gpsimd.tensor_tensor(y_row[:, :], token_out[:, :], no_shift[:, :], ALU.add)
                    pool.drain()
                    nc.gpsimd.indirect_dma_start(
                        out, bass.IndirectOffsetOnAxis(ap=y_row[:, 0:1], axis=0), y[:, :], None,
                        bounds_check=TOKENS + P - 1, oob_is_err=True, compute_op=ALU.add,
                    ).then_inc(y_added, 16)
                    pool.wait_ge(y_added, g * 16 + 16)
                    nc.gpsimd.tensor_tensor(told[:, :], no_shift[:, :], no_shift[:, :], ALU.add).then_inc(y_free, 1)
                    pool.drain()

            with pool.Fori(0, E - 1) as e:
                for q in range(GROUPS):
                    pool.wait_ge(lo_set[q], OPS * e + OPS)
                    pool.dma_start(raw[:, q, :], w_groups[bass.ds(e + 1, 1), q, :, :].squeeze(0)).then_inc(raw_in[q], 16)
                add_blocks(e)
            add_blocks(E - 1)
            end = pool.value_load(table[0:1, 2 * E - 1:2 * E], min_val=1, max_val=MOST_BLOCKS)
            pool.wait_ge(y_added, end * 16)

        @block.tensor
        def _(pe):
            pe.wait_ge(wqk_in, 32)
            pe.wait_ge(ctx_in, 16)
            with pe.Fori(0, B) as b:
                nc.tensor.matmul(bank[4][:, :], wq[:, :], ctx_sb[:, bass.ds(b, 1), :].squeeze(1), start=True, stop=True)
                nc.tensor.matmul(bank[5][:, :], wk[:, :], ctx_sb[:, bass.ds(b, 1), :].squeeze(1), start=True, stop=True).then_inc(qk_mm, 1)
                pe.wait_ge(qk_out, b * 2 + 2)
                for i in range(TB):
                    nc.tensor.matmul(bank[i][:, :], QT[:, i * P:(i + 1) * P], KT[:, :], start=True, stop=True).then_inc(sim_mm, 1)
            pe.wait_ge(settled_set, 1)
            pe.wait_ge(consts, 1)
            nc.tensor.matmul(settled_ps, ones_f[:, :], settled[:, :], start=True, stop=True).then_inc(settled_mm, 1)

            def add_transposed(b):
                At = A[b % 2]
                pe.wait_ge(A_set, b + 1)
                if b > 0:
                    pe.wait_ge(x1_set, TB * b)
                for i in range(TB):
                    nc.tensor.matmul(bank[i][:, :], ident[:, :], At[:, i, :], start=True, stop=False)
                    for j in range(TB):
                        last = nc.tensor.matmul(bank[i][:, j * P:(j + 1) * P], At[:, j, i * P:(i + 1) * P],
                                                ident[:, :], start=False, stop=(j == TB - 1))
                    last.then_inc(AA_mm, 1)

            def scores(b):
                pe.wait_ge(rows_set, b + 1)
                if b == 0:
                    pe.wait_ge(gate_in, 16)

                def transpose_tile(i):
                    if TB * b + i >= 2:
                        pe.wait_ge(xfT_out, TB * b + i - 1)
                    for c in range(DC):
                        last = nc.tensor.transpose(bank[4 + i % 2][:, c * P:(c + 1) * P], rows[:, i, c * P:(c + 1) * P], ident[:, :])
                    last.then_inc(xfT_mm, 1)

                transpose_tile(0)
                for i in range(TB):
                    if i + 1 < TB:
                        transpose_tile(i + 1)
                    pe.wait_ge(xfT_out, TB * b + i + 1)
                    for c in range(DC):
                        last = nc.tensor.matmul(scores_ps[:, i, :], xfT[i % 2][:, c * P:(c + 1) * P], gate_w[:, c, :],
                                                start=(c == 0), stop=(c == DC - 1))
                    last.then_inc(scores_mm, 1)

            def ranks(b):
                pe.wait_ge(mask_set, b + 1)
                for i in range(TB):
                    nc.tensor.matmul(rank_ps[:, i, :], upper[:, :], mask[:, i, :], start=True, stop=False)
                    for j in range(i):
                        nc.tensor.matmul(rank_ps[:, i, :], ones_b[:, :], mask[:, j, :], start=False, stop=False)
                    last = nc.tensor.matmul(rank_ps[:, i, :], ones_b[:, :], before[:, b, :], start=False, stop=True)
                last.then_inc(rank_mm, 1)

            add_transposed(0)
            add_transposed(1)
            scores(0)
            for b in range(2, B):
                ranks(b - 2)
                add_transposed(b)
                scores(b - 1)
            ranks(B - 2)
            scores(B - 1)
            ranks(B - 1)
            nc.tensor.matmul(total_ps, ones_b[:, :], before[:, B, :], start=True, stop=True).then_inc(total_mm, 1)

            def three(out_ap, hi, lo, hi_w, lo_w, start, stop):
                nc.tensor.matmul(out_ap, hi, hi_w, start=start, stop=False)
                nc.tensor.matmul(out_ap, lo, hi_w, start=False, stop=False)
                return nc.tensor.matmul(out_ap, hi, lo_w, start=False, stop=stop)

            def transpose_x(n):
                pe.wait_ge(xtile_in, n * 16)
                for c in range(DC):
                    last = nc.tensor.transpose(bank[X_BANK][:, c * P:(c + 1) * P], xtile[:, c * P:(c + 1) * P], ident[:, :])
                last.then_inc(xT_mm, 1)

            def first_layer(s, which):
                into = (GATE if which == 0 else UP)[s]
                for c in range(DC):
                    cols = slice(which * COLS, (which + 1) * COLS)
                    last = three(bank[into][:, :], xT_hi[:, c, :], xT_lo[:, c, :], w_hi[s][:, c, cols], w_lo[s][:, c, cols],
                                 c == 0, c == DC - 1)
                last.then_inc((gate_mm if which == 0 else up_mm)[s], 1)

            def transpose_h(s):
                for c in range(DC):
                    last = nc.tensor.transpose(bank[H_BANK[s]][:, c * P:(c + 1) * P], h[:, s, c * P:(c + 1) * P], ident[:, :])
                last.then_inc(hT_mm[s], 1)

            def second_layer(chunks):
                for k in chunks:
                    s, cols = k // DC, slice(k % DC * P, (k % DC + 1) * P)
                    w_cols = slice(k % 2 * COLS, (k % 2 + 1) * COLS)
                    last = three(bank[Y_BANK][:, :], hT_hi[:, s, cols], hT_lo[:, s, cols], w_hi[2][:, k // 2, w_cols],
                                 w_lo[2][:, k // 2, w_cols], k == 0, k == IC - 1)
                return last

            pe.wait_ge(table_set, 1)
            transpose_x(1)
            with pe.Fori(0, E) as e:
                split = pe.snap(e * OPS + OPS)
                with blocks(pe, e) as g:
                    nth = pe.snap(g + 1)
                    pe.wait_ge(xT_set, nth)
                    pe.wait_ge(lo_set[0], split)
                    first_layer(0, 0)
                    first_layer(0, 1)
                    pe.wait_ge(lo_set[1], split)
                    first_layer(1, 0)
                    pe.wait_ge(h_set[0], nth)
                    transpose_h(0)
                    first_layer(1, 1)
                    transpose_x(nth + 1)
                    pe.wait_ge(hT_set[0], nth)
                    pe.wait_ge(lo_set[2], split)
                    pe.wait_ge(y_out, nth)
                    second_layer([0])
                    pe.wait_ge(h_set[1], nth)
                    transpose_h(1)
                    second_layer([1, 2, 3])
                    pe.wait_ge(hT_set[1], nth)
                    second_layer([4, 5, 6, 7]).then_inc(y_mm, 1)

        @block.scalar
        def _(act):
            nc.scalar.preload_act_table(ACT.Sigmoid)
            act.wait_ge(gain_in_s, 16)
            nc.scalar.activation(tanh_x, gain_in[:, 0:1], ACT.Tanh)
            nc.scalar.activation(gamma, gain_in[:, 1:2], ACT.Sigmoid)
            nc.scalar.activation(tanh_f, gain_in[:, 2:3], ACT.Tanh).then_inc(gains_act, 1)
            with act.Fori(0, B) as b:
                act.wait_ge(qk_mm, b + 1)
                nc.scalar.activation(QT, bank[4][:, :], ACT.Copy).then_inc(qk_out, 1)
                act.wait_ge(sim_mm, b * TB + TB)
                S_b = S[:, bass.ds(b * TB, TB), :]
                for i in range(TB):
                    last = nc.scalar.activation(S_b[:, i, :], bank[i][:, :], ACT.Copy)
                last.then_inc(sim_out, 1)
            with act.Fori(0, SEARCH) as k:
                for half in range(2):
                    act.wait_ge(probe_set[half], k + 1)
                    for n in range(ON_VECTOR, HALF):
                        t = half * HALF + n
                        last = nc.scalar.activation(signs[half * (HALF - ON_VECTOR) + n - ON_VECTOR], S[:, t, :], ACT.Sign, bias=probe[:, t, 0:1], scale=-1.0,
                                                    accum_out=act_sum[:, t:t + 1])
                    last.then_inc(act_counted[half], 1)

            def split_high(q, steps):
                for j in steps:
                    nc.scalar.activation(w_hi[q][:, j, :], raw[:, q, j * OPW:(j + 1) * OPW], ACT.Copy).then_inc(hi_set[q], 1)

            for q in range(2):
                act.wait_ge(raw_in_0[q], 16)
                split_high(q, range(OPS))

            def sigmoids(b):
                if b >= 2:
                    act.wait_ge(AA_mm, TB * (b - 1))
                act.wait_ge(thr_set, 1)
                nc.scalar.activation(A[b % 2], S[:, b * TB:(b + 1) * TB, :], ACT.Sigmoid, scale=SIM_SCALE).then_inc(sig_set, 1)

            def xfT_copies(b):
                for i in range(TB):
                    act.wait_ge(xfT_mm, TB * b + i + 1)
                    if TB * b + i >= 2:
                        act.wait_ge(scores_mm, TB * b + i - 1)
                    nc.scalar.activation(xfT[i % 2], bank[4 + i % 2][:, :], ACT.Copy).then_inc(xfT_out, 1)

            def shares(b):
                act.wait_ge(lead_set, b + 1)
                nc.scalar.activation(share[:, :, :], lead[:, :, :], ACT.Sigmoid).then_inc(share_set, 1)

            sigmoids(0)
            sigmoids(1)
            xfT_copies(0)
            for b in range(2, B):
                sigmoids(b)
                shares(b - 2)
                xfT_copies(b - 1)
            shares(B - 2)
            xfT_copies(B - 1)
            shares(B - 1)

            nc.scalar.preload_act_table(ACT.Silu)
            act.wait_ge(total_mm, 1)
            act.wait_ge(raw_in_0[2], 16)
            split_high(2, range(OPS))

            def x_high(n):
                act.wait_ge(xT_mm, n)
                nc.scalar.activation(xT_hi[:, :, :], bank[X_BANK][:, :].rearrange("p (c n) -> p c n", c=DC), ACT.Copy).then_inc(xhi_set, 1)

            def silu(s, nth):
                act.wait_ge(gate_mm[s], nth)
                nc.scalar.activation(act_g[:, s, :], bank[GATE[s]][:, :], ACT.Silu).then_inc(silu_set[s], 1)

            def h_high(s, nth):
                act.wait_ge(hT_mm[s], nth)
                nc.scalar.activation(hT_hi[:, s, :], bank[H_BANK[s]][:, :], ACT.Copy).then_inc(hhi_set[s], 1)

            act.wait_ge(table_set, 1)
            x_high(1)
            with act.Fori(0, E) as e:
                change = entry(act, 2, e, 0, 1 << 20)
                arrived = act.snap(e * 16 + 16)
                with blocks(act, e) as g:
                    nth = act.snap(g + 1)
                    silu(0, nth)
                    silu(1, nth)
                    h_high(0, nth)
                    with act.If(g == change):
                        act.wait_ge(up_mm[0], nth)
                        act.wait_ge(raw_in[0], arrived)
                        split_high(0, range(2))
                    with act.Else():
                        act.nop()
                    x_high(nth + 1)
                    h_high(1, nth)
                    with act.If(g == change):
                        split_high(0, range(2, OPS))
                        act.wait_ge(up_mm[1], nth)
                        act.wait_ge(raw_in[1], arrived)
                        split_high(1, range(OPS))
                        act.wait_ge(y_mm, nth)
                        act.wait_ge(raw_in[2], arrived)
                        split_high(2, range(OPS))
                    with act.Else():
                        act.nop()
                    act.nop()

        @block.vector
        def _(dve):
            V = nc.vector
            dve.wait_ge(gains_act, 1)
            V.tensor_tensor(small[:, 1:2], tanh_x, gamma, ALU.mult)
            dve.drain()
            V.tensor_tensor(c1, tanh_x, small[:, 1:2], ALU.subtract)
            V.tensor_scalar(c2, small[:, 1:2], 0.5, None, ALU.mult)
            dve.drain()
            V.tensor_scalar(neg_c1, c1, -1.0, None, ALU.mult).then_inc(gains_set, 1)

            with dve.Fori(0, B) as b:
                dve.wait_ge(qk_mm, b + 1)
                V.tensor_copy(KT, bank[5][:, :]).then_inc(qk_out, 1)
                dve.wait_ge(sim_out, b + 1)
                S_b = S[:, bass.ds(b * TB, TB), :]
                st_b = sim_stats[:, bass.ds(b, 1), :, :].squeeze(1)
                for i in range(TB):
                    V.bn_stats(st_b[:, i, :], S_b[:, i, :])
            dve.drain()
            for t in range(TILES):
                last = V.bn_aggr(sim_mv[:, t, :], sim_stats[:, t // TB, t % TB, :])
            last.then_inc(sim_moments, 1)
            V.memset(low[:, :, 1], 360.0)
            V.memset(high[:, :, 1], 20.0)
            dve.wait_ge(sd_set, 1)
            V.scalar_tensor_tensor(probe[:, :, 0], sim_sd[:, :], 0.5, sim_mv[:, :, 0], ALU.mult, ALU.add)
            V.scalar_tensor_tensor(low[:, :, 0], sim_sd[:, :], -0.66, sim_mv[:, :, 0], ALU.mult, ALU.add)
            V.scalar_tensor_tensor(high[:, :, 0], sim_sd[:, :], 1.54, sim_mv[:, :, 0], ALU.mult, ALU.add).then_inc(probe_set[0], 1)
            V.memset(small[:, 2:3], 0.0).then_inc(probe_set[1], 1)
            dve.drain()

            with dve.Fori(0, SEARCH) as k:
                for half in range(2):
                    ts = slice(half * HALF, (half + 1) * HALF)
                    for n in range(ON_VECTOR):
                        t = half * HALF + n
                        V.tensor_scalar(flags[n], S[:, t, :], probe[:, t, 0:1], None, ALU.is_ge, ALU.add,
                                        accum_out=probe[:, t, 1:2])
                    dve.wait_ge(act_counted[half], k + 1)
                    at = slice(half * HALF + ON_VECTOR, (half + 1) * HALF)
                    V.tensor_scalar(probe[:, at, 1], act_sum[:, at], -0.5, N / 2.0, ALU.mult, ALU.add)
                    dve.drain()
                    counts = probe[:, ts, 1:2].to_broadcast([P, HALF, 2])
                    V.tensor_scalar(is_low[:, :, :], counts, float(KTH), None, ALU.is_ge)
                    V.tensor_scalar(is_high[:, :, :], counts, float(KTH), None, ALU.is_lt)
                    dve.drain()
                    V.copy_predicated(low[:, ts, :], is_low[:, :, :], probe[:, ts, :])
                    V.copy_predicated(high[:, ts, :], is_high[:, :, :], probe[:, ts, :])
                    dve.drain()
                    V.tensor_tensor(span[:, :, :], low[:, ts, :], high[:, ts, :], ALU.subtract)
                    V.tensor_scalar(frac[:, :], low[:, ts, 1], -AIM, None, ALU.add)
                    dve.drain()
                    V.reciprocal(inv[:, :], span[:, :, 1])
                    dve.drain()
                    V.tensor_tensor(frac[:, :], frac[:, :], inv[:, :], ALU.mult)
                    dve.drain()
                    V.tensor_scalar(frac[:, :], frac[:, :], 0.05, 0.95, ALU.max, ALU.min)
                    dve.drain()
                    V.tensor_tensor(frac[:, :], frac[:, :], span[:, :, 0], ALU.mult)
                    dve.drain()
                    V.tensor_tensor(probe[:, ts, 0], low[:, ts, 0], frac[:, :], ALU.subtract).then_inc(probe_set[half], 1)
                    dve.drain()
            V.tensor_scalar(in_window[:, :], high[:, :, 1], float(KTH - WINDOW), None, ALU.is_ge)
            dve.drain()
            V.copy_predicated(probe[:, :, 0], in_window[:, :], high[:, :, 0])
            dve.drain()
            def count_up(t):
                V.tensor_scalar(flags[t % 2], S[:, t, :], probe[:, t, 0:1], None, ALU.is_ge, ALU.add, accum_out=count[:, t:t + 1])

            count_up(0)
            for t in range(TILES):
                dve.drain()
                V.scalar_tensor_tensor(masked[t % 2], flags[t % 2], -BIG, S[:, t, :], ALU.mult, ALU.add)
                if t + 1 < TILES:
                    count_up(t + 1)
                dve.drain()
                V.max(top8[:, t, :], masked[t % 2])
            V.tensor_scalar(count[:, :], count[:, :], -1.0, float(KTH), ALU.mult, ALU.add)
            dve.drain()
            V.tensor_tensor(pick[:, :, :], rank8[:, :, :], count[:, :].unsqueeze(2).to_broadcast([P, TILES, 8]), ALU.is_equal)
            dve.drain()
            V.tensor_reduce(settled[:, :], pick[:, :, :], AX.XY, ALU.add).then_inc(settled_set, 1)
            dve.drain()
            V.tensor_tensor(pick[:, :, :], pick[:, :, :], top8[:, :, :], ALU.mult)
            dve.drain()
            V.tensor_reduce(thr[:, :], pick[:, :, :], AX.X, ALU.add)
            dve.wait_ge(settled_mm, 1)
            V.tensor_copy(settled_i[:, :], settled_ps)
            dve.drain()
            rows_settled = dve.value_load(settled_i[0:1, 0:1], min_val=0, max_val=TOKENS)
            with dve.If(rows_settled < TOKENS):
                with dve.Fori(0, TILES) as t:
                    V.tensor_copy(left_over, S[:, bass.ds(t, 1), :].squeeze(1))
                    dve.drain()
                    with dve.Fori(0, (KTH - 1) // 8):
                        V.max(max8[:, :], left_over)
                        dve.drain()
                        V.match_replace(left_over, max8[:, :], left_over, -BIG)
                        dve.drain()
                    V.max(max8[:, :], left_over)
                    dve.drain()
                    r = (KTH - 1) % 8
                    V.tensor_copy(thr[:, bass.ds(t, 1)], max8[:, r:r + 1])
                    dve.drain()
            with dve.Else():
                dve.nop()
            V.memset(small[:, 3:4], 0.0).then_inc(thr_set, 1)
            dve.drain()

            def stats(k, b, done):
                for i in range(TB):
                    V.bn_stats(ln_stats[:, i, :], xb[:, b % 2, i, :])
                dve.drain()
                for i in range(TB):
                    last = V.bn_aggr(ln_mv[:, k, i, :], ln_stats[:, i, :])
                last.then_inc(done, 1)
                dve.drain()

            def x_stats(b):
                if b > 0:
                    dve.wait_ge(base_set, TB * b)
                dve.wait_ge(x_in[b % 2], 16 * (b // 2 + 1))
                stats(0, b, ln1_stats)

            def mask_A(b):
                dve.wait_ge(sig_set, b + 1)
                for i in range(TB):
                    t = b * TB + i
                    last = V.scalar_tensor_tensor(A[b % 2][:, i, :], S[:, t, :], thr[:, t:t + 1], A[b % 2][:, i, :],
                                                  ALU.is_ge, ALU.mult)
                last.then_inc(A_set, 1)

            def x1(b):
                for i in range(TB):
                    dve.wait_ge(AA_mm, TB * b + i + 1)
                    dve.wait_ge(base_set, TB * b + i + 1)
                    V.scalar_tensor_tensor(xb[:, b % 2, i, :], bank[i][:, :], c2, xb[:, b % 2, i, :],
                                           ALU.mult, ALU.add).then_inc(x1_set, 1)
                dve.drain()
                if b > 0:
                    dve.wait_ge(rows_set, b)
                stats(1, b, ln2_stats)

            def choose(b):
                dve.wait_ge(scores_mm, TB * (b + 1))
                V.tensor_copy(score[:, :, :], scores_ps)
                dve.drain()
                for i in range(TB):
                    V.max(best[:, i, :], score[:, i, :])
                dve.drain()
                for i in range(TB):
                    V.max_index(best_at[:, i, :], best[:, i, :], score[:, i, :])
                V.tensor_tensor(lead[:, :, 0], best[:, :, 0], best[:, :, 1], ALU.subtract)
                V.tensor_tensor(lead[:, :, 1], best[:, :, 1], best[:, :, 0], ALU.subtract).then_inc(lead_set, 1)
                dve.drain()
                V.tensor_copy(best_f[:, :, :], best_at[:, :, 0:2])
                dve.drain()
                V.tensor_tensor(chosen[:, :, :, :], expert_no[:, :, :, :], best_f[:, :, :].unsqueeze(3).to_broadcast([P, TB, 2, E]), ALU.is_equal)
                dve.drain()
                V.tensor_tensor(mask[:, :, :], chosen[:, :, 0, :], chosen[:, :, 1, :], ALU.add)
                V.tensor_reduce(mask_sum[:, :], chosen[:, :, :, :].rearrange("p i k e -> p e (i k)"), AX.X, ALU.add)
                dve.drain()
                V.tensor_tensor(before[:, b + 1, :], before[:, b, :], mask_sum[:, :], ALU.add).then_inc(mask_set, 1)
                dve.wait_ge(share_set, b + 1)
                V.tensor_scalar(share[:, :, :], share[:, :, :], tanh_f, None, ALU.mult)
                dve.drain()
                V.tensor_tensor(weighed[:, :, :, :], chosen[:, :, :, :], share[:, :, :].unsqueeze(3).to_broadcast([P, TB, 2, E]), ALU.mult)
                dve.drain()
                V.tensor_tensor(rows[:, :, META:META + E], weighed[:, :, 0, :], weighed[:, :, 1, :], ALU.add)
                V.tensor_copy(rows[:, :, ROW - 1].bitcast(I32), token_no[:, b * TB:(b + 1) * TB])
                dve.wait_ge(rank_mm, b + 1)
                V.tensor_tensor(place[:, :, :], rank_ps, region_row[:, :, :], ALU.add)
                dve.drain()
                V.tensor_tensor(place_of[:, :, :, :], chosen[:, :, :, :], place[:, :, :].unsqueeze(2).to_broadcast([P, TB, 2, E]), ALU.mult)
                dve.drain()
                V.tensor_reduce(place_f[:, :, :], place_of[:, :, :, :], AX.X, ALU.add)
                dve.drain()
                V.tensor_copy(place_i[:, :, :], place_f[:, :, :]).then_inc(place_set, 1)

            def split_low(q, n, steps):
                for j in steps:
                    dve.wait_ge(hi_set[q], (n - 1) * OPS + j + 1)
                    V.tensor_tensor(w_lo[q][:, j, :], raw[:, q, j * OPW:(j + 1) * OPW], w_hi[q][:, j, :].bitcast(F32),
                                    ALU.subtract).then_inc(lo_set[q], 1)

            x_stats(0)
            mask_A(0)
            for b in range(B):
                if b + 1 < B:
                    x_stats(b + 1)
                    mask_A(b + 1)
                if b > 0:
                    choose(b - 1)
                x1(b)
            split_low(0, 1, range(OPS))
            choose(B - 1)

            dve.wait_ge(total_mm, 1)
            V.tensor_tensor(pad_f[:, :], total_ps, pad_row[:, :], ALU.add)
            V.tensor_scalar(blk_f[:, :], total_ps, float(P - 1), None, ALU.add)
            dve.drain()
            V.tensor_copy(pad_at[:, :], pad_f[:, :]).then_inc(pad_set, 1)
            V.tensor_copy(blk_i[:, :], blk_f[:, :])
            dve.drain()
            V.tensor_single_scalar(blk_j[:, :], blk_i[:, :], 7, ALU.logical_shift_right)
            dve.drain()
            V.tensor_copy(blk_f[:, :], blk_j[:, :])
            V.memset(blk_1[:, :], 1.0)
            dve.drain()
            V.tensor_scalar(table_f[:, 3 * E:4 * E], blk_f[:, :], 1.0, None, ALU.max)
            dve.drain()
            V.tensor_tensor_scan(table_f[:, E:2 * E], blk_1[:, :], table_f[:, 3 * E:4 * E], 0.0, ALU.mult, ALU.add)
            dve.drain()
            V.tensor_tensor(table_f[:, 0:E], table_f[:, E:2 * E], table_f[:, 3 * E:4 * E], ALU.subtract)
            V.tensor_scalar(table_f[:, 2 * E:3 * E], table_f[:, E:2 * E], -1.0, None, ALU.add)
            dve.drain()
            V.memset(table_f[:, 3 * E - 1:3 * E], float(1 << 16))
            dve.drain()
            V.tensor_copy(table[0:1, :], table_f[0:1, :]).then_inc(table_set, 1)
            dve.drain()
            V.memset(small[:, 4:5], 0.0).then_inc(xtile_free, 1)
            V.memset(small[:, 5:6], 0.0).then_inc(y_out, 1)

            split_low(1, 1, range(OPS))

            def x_low(n):
                dve.wait_ge(xhi_set, n)
                V.tensor_copy(meta_next[:, :], xtile[:, META:META + E])
                V.tensor_copy(token_next[:, :], xtile[:, ROW - 1:ROW].bitcast(I32)).then_inc(xtile_free, 1)
                V.tensor_tensor(xT_lo[:, :, :], bank[X_BANK][:, :].rearrange("p (c n) -> p c n", c=DC), xT_hi[:, :, :].bitcast(F32),
                                ALU.subtract).then_inc(xT_set, 1)

            def take_meta():
                dve.drain()
                V.tensor_copy(meta_now[:, :], meta_next[:, :])
                V.tensor_copy(token_now[:, :], token_next[:, :])
                dve.drain()

            def product(s, nth):
                dve.wait_ge(silu_set[s], nth)
                dve.wait_ge(up_mm[s], nth)
                V.tensor_tensor(h[:, s, :], bank[UP[s]][:, :], act_g[:, s, :], ALU.mult).then_inc(h_set[s], 1)

            def h_low(s, nth):
                dve.wait_ge(hhi_set[s], nth)
                V.tensor_tensor(hT_lo[:, s, :], bank[H_BANK[s]][:, :], hT_hi[:, s, :].bitcast(F32), ALU.subtract).then_inc(hT_set[s], 1)

            x_low(1)
            take_meta()
            split_low(2, 1, range(OPS))
            with dve.Fori(0, E) as e:
                change = entry(dve, 2, e, 0, 1 << 20)
                after = dve.snap(e + 2)
                with blocks(dve, e) as g:
                    nth = dve.snap(g + 1)
                    product(0, nth)
                    h_low(0, nth)
                    product(1, nth)
                    with dve.If(g == change):
                        split_low(0, after, range(2))
                    with dve.Else():
                        dve.nop()
                    x_low(nth + 1)
                    h_low(1, nth)
                    with dve.If(g == change):
                        split_low(0, after, range(2, OPS))
                        split_low(1, after, range(OPS))
                    with dve.Else():
                        dve.nop()
                    dve.wait_ge(y_mm, nth)
                    dve.wait_ge(y_free, nth)
                    V.tensor_scalar(y[:, :], bank[Y_BANK][:, :], meta_now[:, bass.ds(e, 1)], None, ALU.mult).then_inc(y_out, 1)
                    V.tensor_copy(token_out[:, :], token_now[:, :]).then_inc(y_set, 1)
                    take_meta()
                    with dve.If(g == change):
                        split_low(2, after, range(OPS))
                    with dve.Else():
                        dve.nop()
                    dve.nop()


def kernel(x, ctx_512, g_xattn, g_ffn, L0_xattn_Wq, L0_xattn_Wk, L0_xattn_gamma_raw, L0_ffn_gate_w,
           L0_ffn_w1, L0_ffn_w2, L0_ffn_w3):
    import numpy as np
    import concourse.bacc as bacc
    from concourse.bass_utils import run_bass_kernel_spmd

    def plain(a):
        return np.ascontiguousarray(np.asarray(a))

    w1, w2, w3 = (plain(a) for a in (L0_ffn_w1, L0_ffn_w2, L0_ffn_w3))
    first = np.stack([w1, w3], axis=0).reshape(2, E, 2, COLS, DC, P).transpose(1, 5, 2, 4, 0, 3)
    second = w2.reshape(E, D, IC, P).transpose(0, 3, 2, 1)
    arrays = {
        "x": plain(x).reshape(TOKENS, D),
        "ctxT": plain(plain(ctx_512).transpose(2, 0, 1)),
        "wqT": plain(plain(L0_xattn_Wq).T),
        "wkT": plain(plain(L0_xattn_Wk).T),
        "gateT": plain(plain(L0_ffn_gate_w).T.reshape(DC, P, E).transpose(1, 0, 2)),
        "weights": plain(np.concatenate([first.reshape(E, P, -1), second.reshape(E, P, -1)], axis=2)),
        "gains": plain(np.concatenate([plain(a).reshape(-1) for a in (g_xattn, L0_xattn_gamma_raw, g_ffn)])),
    }
    nc = bacc.Bacc("TRN2", target_bir_lowering=False, num_devices=1)
    aps = [nc.dram_tensor(k, a.shape, mybir.dt.from_np(a.dtype), kind="ExternalInput").ap() for k, a in arrays.items()]
    out = nc.dram_tensor("out", (TOKENS + P, D), F32, kind="ExternalOutput").ap()
    build(nc, *aps, out)
    result = run_bass_kernel_spmd(nc, [arrays], core_ids=[0])
    return result.results[0]["out"][0:TOKENS].reshape(B, N, D)
```

```python
from contextlib import ExitStack

import concourse.bass as bass
from concourse import mybir

F32 = mybir.dt.float32
F32R = mybir.dt.float32r
BF16 = mybir.dt.bfloat16
I8 = mybir.dt.int8
I32 = mybir.dt.int32
U32 = mybir.dt.uint32
ALU = mybir.AluOpType
ACT = mybir.ActivationFunctionType
AX = mybir.AxisListType

P = 128
B, N, D = 4, 512, 512
TOKENS = B * N
TB = N // P
TILES = B * TB
HALF = TILES // 2
KTH = int(N * 0.3)
SIM_SCALE = 1.0 / (32.0 ** 0.5 * 4.0)
EPS = 1e-5
XBUFS = 3
E, I = 8, 1024
DC = D // P
IC = I // P
COLS = 512
REGION = TOKENS + P
META = D
ROW = D + E + 1
GROUPS, OPS, OPW = 3, 4, 1024
SEARCH = 4
ON_VECTOR = 3
WINDOW = 8
AIM = KTH - (WINDOW + 1) / 2
BIG = 3.0e38
W2_BY_ACT = 2
MOST_BLOCKS = 2 * TOKENS // P + E


def build(nc, x, ctxT, wqT, wkT, gateT, weights, gains, out):
    routed = nc.dram_tensor("routed", (E * REGION, ROW), F32).ap()
    x_tiles = x.rearrange("(b i p) d -> b p i d", p=P, i=TB)
    out_tiles = out[0:TOKENS, :].rearrange("(b i p) d -> b p i d", p=P, i=TB)
    w_groups = weights.rearrange("e p (q n) -> e q p n", q=GROUPS)

    stack = ExitStack()
    with stack:
        def sb(name, shape, dt=F32, on=stack):
            return on.enter_context(nc.sbuf_tensor(name, shape, dt))

        def sem(name):
            return stack.enter_context(nc.semaphore(name))

        raw = sb("raw", [P, GROUPS, OPS * OPW])
        w_hi = [sb(f"w{q}_hi", [P, OPS, OPW], F32R) for q in range(2)]
        w_lo = [sb(f"w{q}_lo", [P, OPS, OPW], F32R) for q in range(2)]
        ident = sb("ident", [P, P])
        meta_next = sb("meta_next", [P, E])
        meta_now = sb("meta_now", [P, E])
        token_next = sb("token_next", [P, 1], I32)
        token_now = sb("token_now", [P, 1], I32)
        token_out = sb("token_out", [P, 1], I32)
        y_row = sb("y_row", [P, 1], I32)
        no_shift = sb("no_shift", [P, 1], I32)
        arrived = sb("arrived", [P, 1], I32)
        table = sb("table", [1, 5 * E], I32)
        pad = sb("pad", [P, ROW])

        part1 = ExitStack()
        S = sb("S", [P, TILES, N], F32, part1)
        work = sb("work", [P, 4096 + TB * ROW + 2 * D], F32, part1)
        xb_own = sb("xb_own", [P, XBUFS - 1, TB, D], F32, part1)
        rows_own = sb("rows_own", [P, TB, ROW], F32, part1)
        wq = sb("wq", [P, P], F32, part1)
        wk = sb("wk", [P, P], F32, part1)
        gate_w = sb("gate_w", [P, DC, E], F32, part1)
        upper = sb("upper", [P, P], BF16, part1)
        ones_b = sb("ones_b", [P, P], BF16, part1)
        ones_f = sb("ones_f", [P, 1], F32, part1)
        gain_in = sb("gain_in", [P, 3], F32, part1)
        gain = sb("gain", [P, 6], F32, part1)
        tanh_x, gamma, tanh_f, c1, c2, neg_c1 = (gain[:, k:k + 1] for k in range(6))
        small = sb("small", [P, 16], F32, part1)
        sim_stats = sb("sim_stats", [P, B, TB, 6], F32, part1)
        sim_mv = sb("sim_mv", [P, TILES, 2], F32, part1)
        sim_sd = sb("sim_sd", [P, TILES], F32, part1)
        half_pow = sb("half_pow", [P, TILES], F32, part1)
        rsqrt_pow = sb("rsqrt_pow", [P, TB], F32, part1)
        low = sb("low", [P, TILES, 2], F32, part1)
        high = sb("high", [P, TILES, 2], F32, part1)
        probe = sb("probe", [P, TILES, 2], F32, part1)
        act_sum = sb("act_sum", [P, TILES], F32, part1)
        is_low = sb("is_low", [P, HALF, 2], I32, part1)
        is_high = sb("is_high", [P, HALF, 2], I32, part1)
        in_window = sb("in_window", [P, TILES], I32, part1)
        span = sb("span", [P, HALF, 2], F32, part1)
        frac = sb("frac", [P, HALF], F32, part1)
        inv = sb("inv", [P, HALF], F32, part1)
        count = sb("count", [P, TILES], F32, part1)
        top8 = sb("top8", [P, TILES, 8], F32, part1)
        rank8 = sb("rank8", [P, TILES, 8], F32, part1)
        pick = sb("pick", [P, TILES, 8], F32, part1)
        thr = sb("thr", [P, TILES], F32, part1)
        settled = sb("settled", [P, 1], F32, part1)
        settled_i = sb("settled_i", [P, 1], I32, part1)
        max8 = sb("max8", [P, 8], F32, part1)
        ln_stats = sb("ln_stats", [P, TB, 6], F32, part1)
        ln_mv = sb("ln_mv", [P, 2, B, TB, 2], F32, part1)
        ln_v = sb("ln_v", [P, 2, B, TB], F32, part1)
        ln_r = sb("ln_r", [P, 2, B, TB], F32, part1)
        ln_m = sb("ln_m", [P, 2, B, TB], F32, part1)
        ln_s = sb("ln_s", [P, B, TB], F32, part1)
        ln_o = sb("ln_o", [P, 2, B, TB], F32, part1)
        score = sb("score", [P, TB, E], F32, part1)
        best = sb("best", [P, TB, 8], F32, part1)
        best_at = sb("best_at", [P, TB, 8], U32, part1)
        best_f = sb("best_f", [P, TB, 2], F32, part1)
        lead = sb("lead", [P, TB, 2], F32, part1)
        share = sb("share", [P, TB, 2], F32, part1)
        expert_no = sb("expert_no", [P, TB, 2, E], F32, part1)
        chosen = sb("chosen", [P, TB, 2, E], F32, part1)
        weighed = sb("weighed", [P, TB, 2, E], F32, part1)
        mask = sb("mask", [P, TB, E], BF16, part1)
        before = sb("before", [P, B + 1, E], BF16, part1)
        mask_sum = sb("mask_sum", [P, E], F32, part1)
        region_row = sb("region_row", [P, TB, E], F32, part1)
        place = sb("place", [P, TB, E], F32, part1)
        place_of = sb("place_of", [P, TB, 2, E], F32, part1)
        place_f = sb("place_f", [P, TB, 2], F32, part1)
        place_i = sb("place_i", [P, 2, TB, 2], I32, part1)
        token_no = sb("token_no", [P, TILES], I32, part1)
        blk_i = sb("blk_i", [P, E], I32, part1)
        blk_j = sb("blk_j", [P, E], I32, part1)
        blk_f = sb("blk_f", [P, E], F32, part1)
        blk_1 = sb("blk_1", [P, E], F32, part1)
        table_f = sb("table_f", [P, 5 * E], F32, part1)
        part1.close()

        xtile = sb("xtile", [P, ROW])
        xT_hi = sb("xT_hi", [P, DC, P], F32R)
        xT_lo = sb("xT_lo", [P, DC, P], F32R)
        hT_hi = sb("hT_hi", [P, 2, COLS], F32R)
        hT_lo = sb("hT_lo", [P, 2, COLS], F32R)
        act_g = sb("act_g", [P, 2, COLS])
        h = sb("h", [P, 2, COLS])
        y = sb("y", [P, D])
        w_hi.append(sb("w2_hi", [P, OPS, OPW], F32R))
        w_lo.append(sb("w2_lo", [P, OPS, OPW], F32R))

        ctx_sb = work[:, 0:2048].rearrange("p (b n) -> p b n", b=B)
        QT, KT = ([work[:, first + 512 * k:first + 512 * (k + 1)] for k in range(2)] for first in (3072, 4096))
        flags = [work[:, 3072 + 256 * k:3328 + 256 * k].bitcast(BF16) for k in range(ON_VECTOR)]
        signs = [work[:, 3840 + 128 * k:3968 + 128 * k].bitcast(I8) for k in range(2 * (HALF - ON_VECTOR))]
        masked = [work[:, 5120 + 512 * k:5632 + 512 * k] for k in range(2)]
        left_over = masked[0]
        A = [work[:, 2048 * k:2048 * (k + 1)].rearrange("p (i n) -> p i n", i=TB) for k in range(2)]
        rows = [rows_own, work[:, 4096:4096 + TB * ROW].rearrange("p (i n) -> p i n", i=TB)]
        xfT = [work[:, 4096 + TB * ROW + D * k:4096 + TB * ROW + D * (k + 1)] for k in range(2)]
        xb = [xb_own[:, k, :, :] for k in range(XBUFS - 1)] + [raw[:, 2, 0:TB * D].rearrange("p (i n) -> p i n", i=TB)]

        bank = [stack.enter_context(nc.psum_tensor(f"bank{k}", [P, COLS], F32)) for k in range(8)]
        GATE, UP, Y_BANK, X_BANK = (0, 2), (1, 3), 7, 6
        H_BANK = (4, 5)
        scores_ps = bank[6][:, 0:TB * E].rearrange("p (i e) -> p i e", e=E)
        rank_ps = bank[7][:, 0:TB * E].rearrange("p (i e) -> p i e", e=E)
        total_ps = bank[0][:, 0:E]
        settled_ps = bank[6][0:1, 64:65]

        wqk_in, gate_in, gain_in_s = sem("wqk_in"), sem("gate_in"), sem("gain_in_s")
        ctx_in = [sem(f"ctx_in{b}") for b in range(B)]
        x_in = [sem(f"x_in{k}") for k in range(XBUFS)]
        raw_in = [sem(f"raw_in{q}") for q in range(GROUPS)]
        raw_in_0 = [sem(f"raw_in_0_{q}") for q in range(GROUPS)]
        consts = sem("consts")
        qk_mm, qk_out, sim_mm, sim_out = sem("qk_mm"), sem("qk_out"), sem("sim_mm"), sem("sim_out")
        sim_moments, sd_set = sem("sim_moments"), sem("sd_set")
        probe_set = [sem("probe_set0"), sem("probe_set1")]
        act_counted = [sem("act_counted0"), sem("act_counted1")]
        settled_set, settled_mm, thr_set = sem("settled_set"), sem("settled_mm"), sem("thr_set")
        gains_act, gains_set = sem("gains_act"), sem("gains_set")
        ln1_stats, ln2_stats, base_set = sem("ln1_stats"), sem("ln2_stats"), sem("base_set")
        ln1_set, ln2_set, pads_in = sem("ln1_set"), sem("ln2_set"), sem("pads_in")
        sig_set, A_set, AA_mm, x1_set = sem("sig_set"), sem("A_set"), sem("AA_mm"), sem("x1_set")
        x1_stored = [sem(f"x1_stored{k}") for k in range(XBUFS)]
        rows_set, xfT_mm, xfT_out, scores_mm = sem("rows_set"), sem("xfT_mm"), sem("xfT_out"), sem("scores_mm")
        lead_set, share_set, mask_set, rank_mm = sem("lead_set"), sem("share_set"), sem("mask_set"), sem("rank_mm")
        place_set, routed_in, total_mm = sem("place_set"), sem("routed_in"), sem("total_mm")
        table_set = sem("table_set")
        hi_set = [sem(f"hi_set{q}") for q in range(GROUPS)]
        lo_set = [sem(f"lo_set{q}") for q in range(GROUPS)]
        xtile_free, y_out = sem("xtile_free"), sem("y_out")
        xtile_in, xT_mm, xhi_set, xT_set = sem("xtile_in"), sem("xT_mm"), sem("xhi_set"), sem("xT_set")
        gate_mm, up_mm = [sem("gate_mm0"), sem("gate_mm1")], [sem("up_mm0"), sem("up_mm1")]
        silu_set, h_set = [sem("silu_set0"), sem("silu_set1")], [sem("h_set0"), sem("h_set1")]
        hT_mm, hhi_set = [sem("hT_mm0"), sem("hT_mm1")], [sem("hhi_set0"), sem("hhi_set1")]
        hT_set = [sem("hT_set0"), sem("hT_set1")]
        y_mm, y_set, y_added = sem("y_mm"), sem("y_set"), sem("y_added")

        def entry(eng, row, e, least, most):
            return eng.value_load(table[0:1, bass.ds(e + row * E, 1)], min_val=least, max_val=most)

        def blocks(eng, e):
            first = entry(eng, 0, e, 0, MOST_BLOCKS - 1)
            end = entry(eng, 1, e, 1, MOST_BLOCKS)
            return eng.Fori(first, end)

        block = stack.enter_context(nc.Block())

        @block.sync
        def _(sp):
            sp.dma_start(wq[:, :], wqT).then_inc(wqk_in, 16)
            sp.dma_start(wk[:, :], wkT).then_inc(wqk_in, 16)
            for b in range(B):
                sp.dma_start(ctx_sb[:, b, :], ctxT[:, b, :]).then_inc(ctx_in[b], 16)
            for b in range(XBUFS):
                sp.dma_start(xb[b][:, :, :], x_tiles[b]).then_inc(x_in[b], 16)
            sp.dma_start(gate_w[:, :, :], gateT).then_inc(gate_in, 16)
            for q in range(2):
                sp.dma_start(raw[:, q, :], w_groups[0, q]).then_inc(raw_in_0[q], 16)
            for b in range(B):
                k = b % XBUFS
                sp.wait_ge(x1_set, TB * (b + 1))
                sp.dma_start(out_tiles[b], xb[k][:, :, :]).then_inc(x1_stored[k], 16)
                if b + XBUFS < B:
                    sp.wait_ge(x1_stored[k], 16)
                    sp.wait_ge(rows_set, b + 1)
                    sp.dma_start(xb[k][:, :, :], x_tiles[b + XBUFS]).then_inc(x_in[k], 16)
            sp.wait_ge(x1_stored[XBUFS - 1], 16)
            sp.wait_ge(rows_set, XBUFS)
            sp.dma_start(raw[:, 2, :], w_groups[0, 2]).then_inc(raw_in_0[2], 16)
            sp.wait_ge(table_set, 1)
            with sp.Fori(0, E) as e:
                at = entry(sp, 4, e, 0, E * REGION - P)
                sp.dma_start(routed[bass.ds(at, P), :], pad[:, :]).then_inc(pads_in, 16)
            sp.wait_ge(routed_in, 16 * 2 * TILES)
            sp.wait_ge(pads_in, 16 * E)
            with sp.Fori(0, E) as e:
                first = entry(sp, 0, e, 0, MOST_BLOCKS - 1)
                some = entry(sp, 3, e, 1, REGION // P)
                with sp.Fori(0, some) as j:
                    sp.wait_ge(xtile_free, first + j + 1)
                    sp.dma_start(xtile[:, :], routed[bass.ds(e * REGION + j * P, P), :]).then_inc(xtile_in, 16)
            end = sp.value_load(table[0:1, 2 * E - 1:2 * E], min_val=1, max_val=MOST_BLOCKS)
            sp.wait_ge(xtile_free, end + 1)
            sp.dma_start(xtile[:, :], routed[0:P, :]).then_inc(xtile_in, 16)

        @block.gpsimd
        def _(pool):
            nc.gpsimd.memset(half_pow[:, :], 0.5)
            nc.gpsimd.memset(rsqrt_pow[:, :], -0.5)
            nc.gpsimd.memset(ident[:, :], 0.0)
            nc.gpsimd.memset(no_shift[:, :], 0)
            nc.gpsimd.memset(upper[:, :], 1.0)
            nc.gpsimd.memset(ones_b[:, :], 1.0)
            nc.gpsimd.memset(ones_f[:, :], 1.0)
            nc.gpsimd.memset(pad[:, :], 0.0)
            nc.gpsimd.memset(before[:, 0, :], 0.0)
            nc.gpsimd.iota(rank8[:, :, :], [[0, TILES], [1, 8]], 1, 0, allow_small_or_imprecise_dtypes=True)
            nc.gpsimd.iota(expert_no[:, :, :, :], [[0, 2 * TB], [1, E]], 0, 0, allow_small_or_imprecise_dtypes=True)
            nc.gpsimd.iota(region_row[:, :, :], [[0, TB], [REGION, E]], 0, 0, allow_small_or_imprecise_dtypes=True)
            nc.gpsimd.iota(token_no[:, :], [[P, TILES]], 0, 1)
            pool.drain()
            nc.gpsimd.affine_select(out=ident[:, :], in_=ident[:, :], compare_op=ALU.not_equal, fill=1.0,
                                    base=0, pattern=[[-1, P]], channel_multiplier=1)
            nc.gpsimd.affine_select(out=upper[:, :], in_=upper[:, :], compare_op=ALU.is_gt, fill=0.0,
                                    base=0, pattern=[[1, P]], channel_multiplier=-1)
            nc.gpsimd.iota(pad[:, ROW - 1:ROW].bitcast(I32), [[0, 1]], TOKENS, 1)
            pool.drain()
            nc.gpsimd.memset(small[:, 0:1], 0.0).then_inc(consts, 1)
            pool.wait_ge(consts, 1)
            pool.dma_start(out[TOKENS:TOKENS + P, :], pad[:, 0:D]).then_inc(y_added, 16)

            pool.wait_ge(sim_moments, 1)
            nc.gpsimd.tensor_tensor(sim_sd[:, :], sim_mv[:, :, 1], half_pow[:, :], ALU.pow).then_inc(sd_set, 1)

            def scales(k, b, stats, done):
                pool.wait_ge(stats, b + 1)
                nc.gpsimd.tensor_scalar(ln_v[:, k, b, :], ln_mv[:, k, b, :, 1], EPS, 1.0, ALU.add, ALU.mult)
                pool.drain()
                nc.gpsimd.tensor_tensor(ln_r[:, k, b, :], ln_v[:, k, b, :], rsqrt_pow[:, :], ALU.pow)
                pool.drain()
                nc.gpsimd.tensor_tensor(ln_m[:, k, b, :], ln_r[:, k, b, :], ln_mv[:, k, b, :, 0], ALU.mult)
                pool.drain()
                if k == 0:
                    nc.gpsimd.tensor_scalar(ln_s[:, b, :], ln_r[:, k, b, :], c1, 1.0, ALU.mult, ALU.add)
                nc.gpsimd.tensor_scalar(ln_o[:, k, b, :], ln_m[:, k, b, :], neg_c1 if k == 0 else -1.0, 1.0,
                                        ALU.mult, ALU.mult).then_inc(done, 1)

            def route(b):
                pool.wait_ge(place_set, b + 1)
                for i in range(TB):
                    for k in range(2):
                        nc.gpsimd.indirect_dma_start(
                            routed, bass.IndirectOffsetOnAxis(ap=place_i[:, b % 2, i, k:k + 1], axis=0),
                            rows[b % 2][:, i, :], None, bounds_check=E * REGION - 1, oob_is_err=True,
                        ).then_inc(routed_in, 16)

            pool.wait_ge(gains_set, 1)
            for b in range(XBUFS):
                scales(0, b, ln1_stats, ln1_set)
                pool.drain()
                for i in range(TB):
                    nc.gpsimd.tensor_scalar(xb[b][:, i, :], xb[b][:, i, :], ln_s[:, b, i:i + 1],
                                            ln_o[:, 0, b, i:i + 1], ALU.mult, ALU.add).then_inc(base_set, 1)
            scales(1, 0, ln2_stats, ln2_set)
            scales(1, 1, ln2_stats, ln2_set)
            for b in range(B):
                route(b)
                if b == 0:
                    for late in range(XBUFS, B):
                        scales(0, late, ln1_stats, ln1_set)
                if b + 2 < B:
                    scales(1, b + 2, ln2_stats, ln2_set)

            pool.wait_ge(table_set, 1)
            pool.wait_ge(y_added, 16)
            for k in range(XBUFS):
                pool.wait_ge(x1_stored[k], 16 * len(range(k, B, XBUFS)))

            def add_blocks(e):
                with blocks(pool, e) as g:
                    pool.wait_ge(y_set, g + 1)
                    nc.gpsimd.tensor_tensor(y_row[:, :], token_out[:, :], no_shift[:, :], ALU.add)
                    pool.drain()
                    nc.gpsimd.indirect_dma_start(
                        out, bass.IndirectOffsetOnAxis(ap=y_row[:, 0:1], axis=0), y[:, :], None,
                        bounds_check=TOKENS + P - 1, oob_is_err=True, compute_op=ALU.add,
                    ).then_inc(y_added, 16)

            def split_w2(e):
                pool.wait_ge(raw_in[2], e * 16 + 16)
                nc.gpsimd.tensor_tensor(arrived[:, :], no_shift[:, :], no_shift[:, :], ALU.add)
                for j in range(OPS):
                    if j < W2_BY_ACT:
                        pool.wait_ge(hi_set[2], e * W2_BY_ACT + OPS + j + 1)
                    else:
                        nc.gpsimd.tensor_scalar(w_hi[2][:, j, :], raw[:, 2, j * OPW:(j + 1) * OPW], 1.0, 1.0, ALU.mult, ALU.mult)
                        pool.drain()
                    nc.gpsimd.tensor_tensor(w_lo[2][:, j, :], raw[:, 2, j * OPW:(j + 1) * OPW], w_hi[2][:, j, :].bitcast(F32),
                                            ALU.subtract).then_inc(lo_set[2], 1)

            with pool.Fori(0, E - 1) as e:
                for q in range(GROUPS):
                    pool.wait_ge(lo_set[q], OPS * e + OPS)
                    pool.dma_start(raw[:, q, :], w_groups[bass.ds(e + 1, 1), q, :, :].squeeze(0)).then_inc(raw_in[q], 16)
                add_blocks(e)
                split_w2(e)
            add_blocks(E - 1)
            end = pool.value_load(table[0:1, 2 * E - 1:2 * E], min_val=1, max_val=MOST_BLOCKS)
            pool.wait_ge(y_added, end * 16 + 16)

        @block.tensor
        def _(pe):
            pe.wait_ge(wqk_in, 32)

            def project(b):
                pe.wait_ge(ctx_in[b], 16)
                nc.tensor.matmul(bank[4 + b % 2 * 2][:, :], wq[:, :], ctx_sb[:, b, :], start=True, stop=True)
                nc.tensor.matmul(bank[5 + b % 2 * 2][:, :], wk[:, :], ctx_sb[:, b, :], start=True, stop=True).then_inc(qk_mm, 1)

            project(0)
            project(1)
            for b in range(B):
                pe.wait_ge(qk_out, b + 1)
                for i in range(TB):
                    if b > 0:
                        pe.wait_ge(sim_out, TB * (b - 1) + i + 1)
                    nc.tensor.matmul(bank[i][:, :], QT[b % 2][:, i * P:(i + 1) * P], KT[b % 2], start=True, stop=True).then_inc(sim_mm, 1)
                if b + 2 < B:
                    project(b + 2)
            pe.wait_ge(settled_set, 1)
            pe.wait_ge(consts, 1)
            nc.tensor.matmul(settled_ps, ones_f[:, :], settled[:, :], start=True, stop=True).then_inc(settled_mm, 1)

            def add_transposed(b, tiles):
                At = A[b % 2]
                pe.wait_ge(A_set, b + 1)
                for i in tiles:
                    if b > 0:
                        pe.wait_ge(x1_set, TB * (b - 1) + i + 1)
                    nc.tensor.matmul(bank[i][:, :], ident[:, :], At[:, i, :], start=True, stop=False)
                    for j in range(TB):
                        last = nc.tensor.matmul(bank[i][:, j * P:(j + 1) * P], At[:, j, i * P:(i + 1) * P],
                                                ident[:, :], start=False, stop=(j == TB - 1))
                    last.then_inc(AA_mm, 1)

            def scores(b):
                pe.wait_ge(rows_set, b + 1)
                if b == 0:
                    pe.wait_ge(gate_in, 16)

                def transpose_tile(i):
                    if TB * b + i >= 2:
                        pe.wait_ge(xfT_out, TB * b + i - 1)
                    for c in range(DC):
                        last = nc.tensor.transpose(bank[4 + i % 2][:, c * P:(c + 1) * P], rows[b % 2][:, i, c * P:(c + 1) * P], ident[:, :])
                    last.then_inc(xfT_mm, 1)

                transpose_tile(0)
                for i in range(TB):
                    if i + 1 < TB:
                        transpose_tile(i + 1)
                    pe.wait_ge(xfT_out, TB * b + i + 1)
                    for c in range(DC):
                        last = nc.tensor.matmul(scores_ps[:, i, :], xfT[i % 2][:, c * P:(c + 1) * P], gate_w[:, c, :],
                                                start=(c == 0), stop=(c == DC - 1))
                    last.then_inc(scores_mm, 1)

            def ranks(b):
                pe.wait_ge(mask_set, b + 1)
                for i in range(TB):
                    nc.tensor.matmul(rank_ps[:, i, :], upper[:, :], mask[:, i, :], start=True, stop=False)
                    for j in range(i):
                        nc.tensor.matmul(rank_ps[:, i, :], ones_b[:, :], mask[:, j, :], start=False, stop=False)
                    last = nc.tensor.matmul(rank_ps[:, i, :], ones_b[:, :], before[:, b, :], start=False, stop=True)
                last.then_inc(rank_mm, 1)

            add_transposed(0, range(TB))
            add_transposed(1, range(TB))
            scores(0)
            for b in range(1, B):
                if b + 1 < B:
                    add_transposed(b + 1, range(TB // 2))
                ranks(b - 1)
                if b + 1 < B:
                    add_transposed(b + 1, range(TB // 2, TB))
                scores(b)
            ranks(B - 1)
            nc.tensor.matmul(total_ps, ones_b[:, :], before[:, B, :], start=True, stop=True).then_inc(total_mm, 1)

            def three(out_ap, hi, lo, hi_w, lo_w, start, stop):
                nc.tensor.matmul(out_ap, hi, hi_w, start=start, stop=False)
                nc.tensor.matmul(out_ap, lo, hi_w, start=False, stop=False)
                return nc.tensor.matmul(out_ap, hi, lo_w, start=False, stop=stop)

            def transpose_x(n):
                pe.wait_ge(xtile_in, n * 16)
                for c in range(DC):
                    last = nc.tensor.transpose(bank[X_BANK][:, c * P:(c + 1) * P], xtile[:, c * P:(c + 1) * P], ident[:, :])
                last.then_inc(xT_mm, 1)

            def first_layer(s, which, c):
                into = (GATE if which == 0 else UP)[s]
                cols = slice(which * COLS, (which + 1) * COLS)
                last = three(bank[into][:, :], xT_hi[:, c, :], xT_lo[:, c, :], w_hi[s][:, c, cols], w_lo[s][:, c, cols],
                             c == 0, c == DC - 1)
                if c == DC - 1:
                    last.then_inc((gate_mm if which == 0 else up_mm)[s], 1)

            def transpose_h(s):
                for c in range(DC):
                    last = nc.tensor.transpose(bank[H_BANK[s]][:, c * P:(c + 1) * P], h[:, s, c * P:(c + 1) * P], ident[:, :])
                last.then_inc(hT_mm[s], 1)

            def second_layer(chunks):
                for k in chunks:
                    s, cols = k // DC, slice(k % DC * P, (k % DC + 1) * P)
                    w_cols = slice(k % 2 * COLS, (k % 2 + 1) * COLS)
                    last = three(bank[Y_BANK][:, :], hT_hi[:, s, cols], hT_lo[:, s, cols], w_hi[2][:, k // 2, w_cols],
                                 w_lo[2][:, k // 2, w_cols], k == 0, k == IC - 1)
                return last

            pe.wait_ge(table_set, 1)
            transpose_x(1)
            with pe.Fori(0, E) as e:
                split = [pe.snap(e * OPS + j + 1) for j in range(OPS)]
                with blocks(pe, e) as g:
                    nth = pe.snap(g + 1)
                    pe.wait_ge(xT_set, nth)
                    for c in range(DC):
                        pe.wait_ge(lo_set[0], split[c])
                        first_layer(0, 0, c)
                        first_layer(0, 1, c)
                    for c in range(2):
                        pe.wait_ge(lo_set[1], split[c])
                        first_layer(1, 0, c)
                        first_layer(1, 1, c)
                    for c in range(2, DC):
                        pe.wait_ge(lo_set[1], split[c])
                        first_layer(1, 0, c)
                    pe.wait_ge(h_set[0], nth)
                    transpose_h(0)
                    for c in range(2, DC):
                        first_layer(1, 1, c)
                    transpose_x(nth + 1)
                    pe.wait_ge(hT_set[0], nth)
                    pe.wait_ge(lo_set[2], split[0])
                    pe.wait_ge(y_out, nth)
                    second_layer([0])
                    pe.wait_ge(h_set[1], nth)
                    transpose_h(1)
                    second_layer([1])
                    pe.wait_ge(lo_set[2], split[1])
                    second_layer([2, 3])
                    pe.wait_ge(hT_set[1], nth)
                    pe.wait_ge(lo_set[2], split[2])
                    second_layer([4, 5])
                    pe.wait_ge(lo_set[2], split[3])
                    second_layer([6, 7]).then_inc(y_mm, 1)

        @block.scalar
        def _(act):
            act.dma_start(gain_in[:, :], gains.partition_broadcast(P)).then_inc(gain_in_s, 16)
            nc.scalar.preload_act_table(ACT.Sigmoid)

            def projected(b):
                act.wait_ge(qk_mm, b + 1)
                if b >= 2:
                    act.wait_ge(sim_mm, TB * (b - 1))
                nc.scalar.activation(QT[b % 2], bank[4 + b % 2 * 2][:, :], ACT.Copy)
                nc.scalar.activation(KT[b % 2], bank[5 + b % 2 * 2][:, :], ACT.Copy).then_inc(qk_out, 1)

            projected(0)
            projected(1)
            for b in range(B):
                for i in range(TB):
                    act.wait_ge(sim_mm, b * TB + i + 1)
                    nc.scalar.activation(S[:, b * TB + i, :], bank[i][:, :], ACT.Copy).then_inc(sim_out, 1)
                if b + 2 < B:
                    projected(b + 2)
            act.wait_ge(gain_in_s, 16)
            nc.scalar.activation(tanh_x, gain_in[:, 0:1], ACT.Tanh)
            nc.scalar.activation(gamma, gain_in[:, 1:2], ACT.Sigmoid)
            nc.scalar.activation(tanh_f, gain_in[:, 2:3], ACT.Tanh).then_inc(gains_act, 1)
            with act.Fori(0, SEARCH) as k:
                for half in range(2):
                    act.wait_ge(probe_set[half], k + 1)
                    for n in range(ON_VECTOR, HALF):
                        t = half * HALF + n
                        last = nc.scalar.activation(signs[half * (HALF - ON_VECTOR) + n - ON_VECTOR], S[:, t, :], ACT.Sign, bias=probe[:, t, 0:1], scale=-1.0,
                                                    accum_out=act_sum[:, t:t + 1])
                    last.then_inc(act_counted[half], 1)

            def split_high(q, steps):
                for j in steps:
                    nc.scalar.activation(w_hi[q][:, j, :], raw[:, q, j * OPW:(j + 1) * OPW], ACT.Copy).then_inc(hi_set[q], 1)

            for q in range(2):
                act.wait_ge(raw_in_0[q], 16)
                split_high(q, range(OPS))

            def sigmoids(b):
                if b >= 2:
                    act.wait_ge(AA_mm, TB * (b - 1))
                act.wait_ge(thr_set, 1)
                nc.scalar.activation(A[b % 2], S[:, b * TB:(b + 1) * TB, :], ACT.Sigmoid, scale=SIM_SCALE).then_inc(sig_set, 1)

            def xfT_copies(b):
                for i in range(TB):
                    act.wait_ge(xfT_mm, TB * b + i + 1)
                    if TB * b + i >= 2:
                        act.wait_ge(scores_mm, TB * b + i - 1)
                    nc.scalar.activation(xfT[i % 2], bank[4 + i % 2][:, :], ACT.Copy).then_inc(xfT_out, 1)

            def normal_rows(b):
                act.wait_ge(ln2_set, b + 1)
                if b >= 2:
                    act.wait_ge(routed_in, 16 * 2 * TB * (b - 1))
                for i in range(TB):
                    last = nc.scalar.activation(rows[b % 2][:, i, 0:D], xb[b % XBUFS][:, i, :], ACT.Identity,
                                                bias=ln_o[:, 1, b, i:i + 1], scale=ln_r[:, 1, b, i:i + 1])
                last.then_inc(rows_set, 1)

            def late_base(b):
                act.wait_ge(ln1_set, b + 1)
                for i in range(TB):
                    nc.scalar.activation(xb[b % XBUFS][:, i, :], xb[b % XBUFS][:, i, :], ACT.Identity,
                                         bias=ln_o[:, 0, b, i:i + 1], scale=ln_s[:, b, i:i + 1]).then_inc(base_set, 1)

            def shares(b):
                act.wait_ge(lead_set, b + 1)
                nc.scalar.activation(share[:, :, :], lead[:, :, :], ACT.Sigmoid).then_inc(share_set, 1)

            for b in range(3):
                sigmoids(b)
            normal_rows(0)
            xfT_copies(0)
            for b in range(1, B):
                if b + 2 < B:
                    sigmoids(b + 2)
                shares(b - 1)
                normal_rows(b)
                xfT_copies(b)
                if b == 1:
                    for late in range(XBUFS, B):
                        late_base(late)
            shares(B - 1)

            nc.scalar.preload_act_table(ACT.Silu)
            act.wait_ge(total_mm, 1)
            act.wait_ge(raw_in_0[2], 16)
            split_high(2, range(OPS))

            def x_high(n):
                act.wait_ge(xT_mm, n)
                nc.scalar.activation(xT_hi[:, :, :], bank[X_BANK][:, :].rearrange("p (c n) -> p c n", c=DC), ACT.Copy).then_inc(xhi_set, 1)

            def silu(s, nth):
                act.wait_ge(gate_mm[s], nth)
                nc.scalar.activation(act_g[:, s, :], bank[GATE[s]][:, :], ACT.Silu).then_inc(silu_set[s], 1)

            def h_high(s, nth):
                act.wait_ge(hT_mm[s], nth)
                nc.scalar.activation(hT_hi[:, s, :], bank[H_BANK[s]][:, :], ACT.Copy).then_inc(hhi_set[s], 1)

            act.wait_ge(table_set, 1)
            x_high(1)
            with act.Fori(0, E) as e:
                change = entry(act, 2, e, 0, 1 << 20)
                arrived = act.snap(e * 16 + 16)
                with blocks(act, e) as g:
                    nth = act.snap(g + 1)
                    silu(0, nth)
                    silu(1, nth)
                    h_high(0, nth)
                    x_high(nth + 1)
                    h_high(1, nth)
                    with act.If(g == change):
                        act.wait_ge(up_mm[0], nth)
                        act.wait_ge(raw_in[0], arrived)
                        split_high(0, range(OPS))
                        act.wait_ge(up_mm[1], nth)
                        act.wait_ge(raw_in[1], arrived)
                        split_high(1, range(OPS))
                        act.wait_ge(y_mm, nth)
                        act.wait_ge(raw_in[2], arrived)
                        split_high(2, range(W2_BY_ACT))
                    with act.Else():
                        act.nop()
                    act.nop()

        @block.vector
        def _(dve):
            V = nc.vector

            def stats(k, b, done):
                for i in range(TB):
                    V.bn_stats(ln_stats[:, i, :], xb[b % XBUFS][:, i, :])
                dve.drain()
                for i in range(TB):
                    last = V.bn_aggr(ln_mv[:, k, b, i, :], ln_stats[:, i, :])
                last.then_inc(done, 1)
                dve.drain()

            def x_stats(b):
                dve.wait_ge(x_in[b % XBUFS], 16 * (b // XBUFS + 1))
                stats(0, b, ln1_stats)

            for b in range(B):
                for i in range(TB):
                    dve.wait_ge(sim_out, TB * b + i + 1)
                    V.bn_stats(sim_stats[:, b, i, :], S[:, TB * b + i, :])
                if 0 < b <= XBUFS:
                    x_stats(b - 1)
            dve.drain()
            for t in range(TILES):
                last = V.bn_aggr(sim_mv[:, t, :], sim_stats[:, t // TB, t % TB, :])
            last.then_inc(sim_moments, 1)
            dve.wait_ge(gains_act, 1)
            V.tensor_tensor(small[:, 1:2], tanh_x, gamma, ALU.mult)
            dve.drain()
            V.tensor_tensor(c1, tanh_x, small[:, 1:2], ALU.subtract)
            V.tensor_scalar(c2, small[:, 1:2], 0.5, None, ALU.mult)
            dve.drain()
            V.tensor_scalar(neg_c1, c1, -1.0, None, ALU.mult).then_inc(gains_set, 1)

            V.memset(low[:, :, 1], 360.0)
            V.memset(high[:, :, 1], 20.0)
            dve.wait_ge(sd_set, 1)
            V.scalar_tensor_tensor(probe[:, :, 0], sim_sd[:, :], 0.5, sim_mv[:, :, 0], ALU.mult, ALU.add)
            V.scalar_tensor_tensor(low[:, :, 0], sim_sd[:, :], -0.66, sim_mv[:, :, 0], ALU.mult, ALU.add)
            V.scalar_tensor_tensor(high[:, :, 0], sim_sd[:, :], 1.54, sim_mv[:, :, 0], ALU.mult, ALU.add).then_inc(probe_set[0], 1)
            V.memset(small[:, 2:3], 0.0).then_inc(probe_set[1], 1)
            dve.drain()

            with dve.Fori(0, SEARCH) as k:
                for half in range(2):
                    ts = slice(half * HALF, (half + 1) * HALF)
                    for n in range(ON_VECTOR):
                        t = half * HALF + n
                        V.tensor_scalar(flags[n], S[:, t, :], probe[:, t, 0:1], None, ALU.is_ge, ALU.add,
                                        accum_out=probe[:, t, 1:2])
                    dve.wait_ge(act_counted[half], k + 1)
                    at = slice(half * HALF + ON_VECTOR, (half + 1) * HALF)
                    V.tensor_scalar(probe[:, at, 1], act_sum[:, at], -0.5, N / 2.0, ALU.mult, ALU.add)
                    dve.drain()
                    counts = probe[:, ts, 1:2].to_broadcast([P, HALF, 2])
                    V.tensor_scalar(is_low[:, :, :], counts, float(KTH), None, ALU.is_ge)
                    V.tensor_scalar(is_high[:, :, :], counts, float(KTH), None, ALU.is_lt)
                    dve.drain()
                    V.copy_predicated(low[:, ts, :], is_low[:, :, :], probe[:, ts, :])
                    V.copy_predicated(high[:, ts, :], is_high[:, :, :], probe[:, ts, :])
                    dve.drain()
                    V.tensor_tensor(span[:, :, :], low[:, ts, :], high[:, ts, :], ALU.subtract)
                    V.tensor_scalar(frac[:, :], low[:, ts, 1], -AIM, None, ALU.add)
                    dve.drain()
                    V.reciprocal(inv[:, :], span[:, :, 1])
                    dve.drain()
                    V.tensor_tensor(frac[:, :], frac[:, :], inv[:, :], ALU.mult)
                    dve.drain()
                    V.tensor_scalar(frac[:, :], frac[:, :], 0.05, 0.95, ALU.max, ALU.min)
                    dve.drain()
                    V.tensor_tensor(frac[:, :], frac[:, :], span[:, :, 0], ALU.mult)
                    dve.drain()
                    V.tensor_tensor(probe[:, ts, 0], low[:, ts, 0], frac[:, :], ALU.subtract).then_inc(probe_set[half], 1)
                    dve.drain()
            V.tensor_scalar(in_window[:, :], high[:, :, 1], float(KTH - WINDOW), None, ALU.is_ge)
            dve.drain()
            V.copy_predicated(probe[:, :, 0], in_window[:, :], high[:, :, 0])
            dve.drain()
            def count_up(t):
                V.tensor_scalar(flags[t % 2], S[:, t, :], probe[:, t, 0:1], None, ALU.is_ge, ALU.add, accum_out=count[:, t:t + 1])

            count_up(0)
            for t in range(TILES):
                dve.drain()
                V.scalar_tensor_tensor(masked[t % 2], flags[t % 2], -BIG, S[:, t, :], ALU.mult, ALU.add)
                if t + 1 < TILES:
                    count_up(t + 1)
                dve.drain()
                V.max(top8[:, t, :], masked[t % 2])
            V.tensor_scalar(count[:, :], count[:, :], -1.0, float(KTH), ALU.mult, ALU.add)
            dve.drain()
            V.tensor_tensor(pick[:, :, :], rank8[:, :, :], count[:, :].unsqueeze(2).to_broadcast([P, TILES, 8]), ALU.is_equal)
            dve.drain()
            V.tensor_reduce(settled[:, :], pick[:, :, :], AX.XY, ALU.add).then_inc(settled_set, 1)
            dve.drain()
            V.tensor_tensor(pick[:, :, :], pick[:, :, :], top8[:, :, :], ALU.mult)
            dve.drain()
            V.tensor_reduce(thr[:, :], pick[:, :, :], AX.X, ALU.add)
            dve.wait_ge(settled_mm, 1)
            V.tensor_copy(settled_i[0:1, :], settled_ps)
            dve.drain()
            rows_settled = dve.value_load(settled_i[0:1, 0:1], min_val=0, max_val=TOKENS)
            with dve.If(rows_settled < TOKENS):
                with dve.Fori(0, TILES) as t:
                    V.tensor_copy(left_over, S[:, bass.ds(t, 1), :].squeeze(1))
                    dve.drain()
                    with dve.Fori(0, (KTH - 1) // 8):
                        V.max(max8[:, :], left_over)
                        dve.drain()
                        V.match_replace(left_over, max8[:, :], left_over, -BIG)
                        dve.drain()
                    V.max(max8[:, :], left_over)
                    dve.drain()
                    r = (KTH - 1) % 8
                    V.tensor_copy(thr[:, bass.ds(t, 1)], max8[:, r:r + 1])
                    dve.drain()
            with dve.Else():
                dve.nop()
            V.memset(small[:, 3:4], 0.0).then_inc(thr_set, 1)
            dve.drain()

            def mask_A(b):
                dve.wait_ge(sig_set, b + 1)
                for i in range(TB):
                    t = b * TB + i
                    last = V.scalar_tensor_tensor(A[b % 2][:, i, :], S[:, t, :], thr[:, t:t + 1], A[b % 2][:, i, :],
                                                  ALU.is_ge, ALU.mult)
                last.then_inc(A_set, 1)

            def x1(b):
                for i in range(TB):
                    dve.wait_ge(AA_mm, TB * b + i + 1)
                    dve.wait_ge(base_set, TB * b + i + 1)
                    V.scalar_tensor_tensor(xb[b % XBUFS][:, i, :], bank[i][:, :], c2, xb[b % XBUFS][:, i, :],
                                           ALU.mult, ALU.add).then_inc(x1_set, 1)
                dve.drain()
                stats(1, b, ln2_stats)

            def choose(b):
                dve.wait_ge(scores_mm, TB * (b + 1))
                V.tensor_copy(score[:, :, :], scores_ps)
                dve.drain()
                for i in range(TB):
                    V.max(best[:, i, :], score[:, i, :])
                dve.drain()
                for i in range(TB):
                    V.max_index(best_at[:, i, :], best[:, i, :], score[:, i, :])
                V.tensor_tensor(lead[:, :, 0], best[:, :, 0], best[:, :, 1], ALU.subtract)
                V.tensor_tensor(lead[:, :, 1], best[:, :, 1], best[:, :, 0], ALU.subtract).then_inc(lead_set, 1)
                dve.drain()
                V.tensor_copy(best_f[:, :, :], best_at[:, :, 0:2])
                dve.drain()
                V.tensor_tensor(chosen[:, :, :, :], expert_no[:, :, :, :], best_f[:, :, :].unsqueeze(3).to_broadcast([P, TB, 2, E]), ALU.is_equal)
                dve.drain()
                V.tensor_tensor(mask[:, :, :], chosen[:, :, 0, :], chosen[:, :, 1, :], ALU.add)
                V.tensor_reduce(mask_sum[:, :], chosen[:, :, :, :].rearrange("p i k e -> p e (i k)"), AX.X, ALU.add)
                dve.drain()
                V.tensor_tensor(before[:, b + 1, :], before[:, b, :], mask_sum[:, :], ALU.add).then_inc(mask_set, 1)
                dve.wait_ge(share_set, b + 1)
                V.tensor_scalar(share[:, :, :], share[:, :, :], tanh_f, None, ALU.mult)
                dve.drain()
                V.tensor_tensor(weighed[:, :, :, :], chosen[:, :, :, :], share[:, :, :].unsqueeze(3).to_broadcast([P, TB, 2, E]), ALU.mult)
                dve.drain()
                V.tensor_tensor(rows[b % 2][:, :, META:META + E], weighed[:, :, 0, :], weighed[:, :, 1, :], ALU.add)
                V.tensor_copy(rows[b % 2][:, :, ROW - 1].bitcast(I32), token_no[:, b * TB:(b + 1) * TB])
                dve.wait_ge(rank_mm, b + 1)
                V.tensor_tensor(place[:, :, :], rank_ps, region_row[:, :, :], ALU.add)
                dve.drain()
                V.tensor_tensor(place_of[:, :, :, :], chosen[:, :, :, :], place[:, :, :].unsqueeze(2).to_broadcast([P, TB, 2, E]), ALU.mult)
                dve.drain()
                V.tensor_reduce(place_f[:, :, :], place_of[:, :, :, :], AX.X, ALU.add)
                dve.drain()
                V.tensor_copy(place_i[:, b % 2, :, :], place_f[:, :, :]).then_inc(place_set, 1)

            def split_low(q, n, steps):
                for j in steps:
                    dve.wait_ge(hi_set[q], (n - 1) * OPS + j + 1)
                    V.tensor_tensor(w_lo[q][:, j, :], raw[:, q, j * OPW:(j + 1) * OPW], w_hi[q][:, j, :].bitcast(F32),
                                    ALU.subtract).then_inc(lo_set[q], 1)

            mask_A(0)
            mask_A(1)
            split_low(0, 1, range(OPS))
            x1(0)
            mask_A(2)
            split_low(1, 1, range(OPS))
            x1(1)
            choose(0)
            for late in range(XBUFS, B):
                x_stats(late)
                mask_A(late)
            for b in range(2, B):
                x1(b)
                choose(b - 1)
            choose(B - 1)

            dve.wait_ge(total_mm, 1)
            V.tensor_tensor(table_f[:, 4 * E:5 * E], total_ps, region_row[:, 0, :], ALU.add)
            V.tensor_scalar(blk_f[:, :], total_ps, float(P - 1), None, ALU.add)
            dve.drain()
            V.tensor_copy(blk_i[:, :], blk_f[:, :])
            dve.drain()
            V.tensor_single_scalar(blk_j[:, :], blk_i[:, :], 7, ALU.logical_shift_right)
            dve.drain()
            V.tensor_copy(blk_f[:, :], blk_j[:, :])
            V.memset(blk_1[:, :], 1.0)
            dve.drain()
            V.tensor_scalar(table_f[:, 3 * E:4 * E], blk_f[:, :], 1.0, None, ALU.max)
            dve.drain()
            V.tensor_tensor_scan(table_f[:, E:2 * E], blk_1[:, :], table_f[:, 3 * E:4 * E], 0.0, ALU.mult, ALU.add)
            dve.drain()
            V.tensor_tensor(table_f[:, 0:E], table_f[:, E:2 * E], table_f[:, 3 * E:4 * E], ALU.subtract)
            V.tensor_scalar(table_f[:, 2 * E:3 * E], table_f[:, E:2 * E], -1.0, None, ALU.add)
            dve.drain()
            V.memset(table_f[:, 3 * E - 1:3 * E], float(1 << 16))
            dve.drain()
            V.tensor_copy(table[0:1, :], table_f[0:1, :]).then_inc(table_set, 1)
            dve.drain()
            V.memset(small[:, 4:5], 0.0).then_inc(xtile_free, 1)
            V.memset(small[:, 5:6], 0.0).then_inc(y_out, 1)

            def x_low(n):
                dve.wait_ge(xhi_set, n)
                V.tensor_copy(meta_next[:, :], xtile[:, META:META + E])
                V.tensor_copy(token_next[:, :], xtile[:, ROW - 1:ROW].bitcast(I32)).then_inc(xtile_free, 1)
                V.tensor_tensor(xT_lo[:, :, :], bank[X_BANK][:, :].rearrange("p (c n) -> p c n", c=DC), xT_hi[:, :, :].bitcast(F32),
                                ALU.subtract).then_inc(xT_set, 1)

            def take_meta():
                dve.drain()
                V.tensor_copy(meta_now[:, :], meta_next[:, :])
                V.tensor_copy(token_now[:, :], token_next[:, :])
                dve.drain()

            def product(s, nth):
                dve.wait_ge(silu_set[s], nth)
                dve.wait_ge(up_mm[s], nth)
                V.tensor_tensor(h[:, s, :], bank[UP[s]][:, :], act_g[:, s, :], ALU.mult).then_inc(h_set[s], 1)

            def h_low(s, nth):
                dve.wait_ge(hhi_set[s], nth)
                V.tensor_tensor(hT_lo[:, s, :], bank[H_BANK[s]][:, :], hT_hi[:, s, :].bitcast(F32), ALU.subtract).then_inc(hT_set[s], 1)

            x_low(1)
            take_meta()
            split_low(2, 1, range(OPS))
            with dve.Fori(0, E) as e:
                change = entry(dve, 2, e, 0, 1 << 20)
                after = dve.snap(e + 2)
                with blocks(dve, e) as g:
                    nth = dve.snap(g + 1)
                    product(0, nth)
                    h_low(0, nth)
                    product(1, nth)
                    x_low(nth + 1)
                    h_low(1, nth)
                    with dve.If(g == change):
                        split_low(0, after, range(3))
                    with dve.Else():
                        dve.nop()
                    dve.wait_ge(y_mm, nth)
                    dve.wait_ge(y_added, g * 16 + 16)
                    V.tensor_scalar(y[:, :], bank[Y_BANK][:, :], meta_now[:, bass.ds(e, 1)], None, ALU.mult).then_inc(y_out, 1)
                    V.tensor_copy(token_out[:, :], token_now[:, :]).then_inc(y_set, 1)
                    take_meta()
                    with dve.If(g == change):
                        split_low(0, after, range(3, OPS))
                        split_low(1, after, range(OPS))
                    with dve.Else():
                        dve.nop()
                    dve.nop()


def kernel(x, ctx_512, g_xattn, g_ffn, L0_xattn_Wq, L0_xattn_Wk, L0_xattn_gamma_raw, L0_ffn_gate_w,
           L0_ffn_w1, L0_ffn_w2, L0_ffn_w3):
    import numpy as np
    import concourse.bacc as bacc
    from concourse.bass_utils import run_bass_kernel_spmd

    def plain(a):
        return np.ascontiguousarray(np.asarray(a))

    w1, w2, w3 = (plain(a) for a in (L0_ffn_w1, L0_ffn_w2, L0_ffn_w3))
    first = np.stack([w1, w3], axis=0).reshape(2, E, 2, COLS, DC, P).transpose(1, 5, 2, 4, 0, 3)
    second = w2.reshape(E, D, IC, P).transpose(0, 3, 2, 1)
    arrays = {
        "x": plain(x).reshape(TOKENS, D),
        "ctxT": plain(plain(ctx_512).transpose(2, 0, 1)),
        "wqT": plain(plain(L0_xattn_Wq).T),
        "wkT": plain(plain(L0_xattn_Wk).T),
        "gateT": plain(plain(L0_ffn_gate_w).T.reshape(DC, P, E).transpose(1, 0, 2)),
        "weights": plain(np.concatenate([first.reshape(E, P, -1), second.reshape(E, P, -1)], axis=2)),
        "gains": plain(np.concatenate([plain(a).reshape(-1) for a in (g_xattn, L0_xattn_gamma_raw, g_ffn)])),
    }
    nc = bacc.Bacc("TRN2", target_bir_lowering=False, num_devices=1)
    aps = [nc.dram_tensor(k, a.shape, mybir.dt.from_np(a.dtype), kind="ExternalInput").ap() for k, a in arrays.items()]
    out = nc.dram_tensor("out", (TOKENS + P, D), F32, kind="ExternalOutput").ap()
    build(nc, *aps, out)
    result = run_bass_kernel_spmd(nc, [arrays], core_ids=[0])
    return result.results[0]["out"][0:TOKENS].reshape(B, N, D)
```

```python
from contextlib import ExitStack

import concourse.bass as bass
from concourse import mybir

F32 = mybir.dt.float32
F32R = mybir.dt.float32r
BF16 = mybir.dt.bfloat16
I8 = mybir.dt.int8
I32 = mybir.dt.int32
U32 = mybir.dt.uint32
ALU = mybir.AluOpType
ACT = mybir.ActivationFunctionType
AX = mybir.AxisListType

P = 128
B, N, D = 4, 512, 512
TOKENS = B * N
TB = N // P
TILES = B * TB
HALF = TILES // 2
KTH = int(N * 0.3)
SIM_SCALE = 1.0 / (32.0 ** 0.5 * 4.0)
EPS = 1e-5
XBUFS = 3
SOON = 2
EARLY = 2
E, I = 8, 1024
DC = D // P
IC = I // P
COLS = 512
REGION = TOKENS + P
META = D
ROW = D + E + 1
GROUPS, OPS, OPW = 3, 4, 1024
SEARCH = 4
ON_VECTOR = 2
WINDOW = 8
AIM = KTH - (WINDOW + 1) / 2
ON_POOL = 12
BIG = 3.0e38
W2_BY_ACT = 3
MOST_BLOCKS = 2 * TOKENS // P + E


def build(nc, x, ctxT, wqT, wkT, gateT, weights, gains, out):
    routed = nc.dram_tensor("routed", (E * REGION, ROW), F32).ap()
    x_tiles = x.rearrange("(b i p) d -> b p i d", p=P, i=TB)
    out_tiles = out[0:TOKENS, :].rearrange("(b i p) d -> b p i d", p=P, i=TB)
    w_groups = weights.rearrange("e p (q n) -> e q p n", q=GROUPS)

    stack = ExitStack()
    with stack:
        def sb(name, shape, dt=F32, on=stack):
            return on.enter_context(nc.sbuf_tensor(name, shape, dt))

        def sem(name):
            return stack.enter_context(nc.semaphore(name))

        raw = sb("raw", [P, GROUPS, OPS * OPW])
        w_hi = [sb(f"w{q}_hi", [P, OPS, OPW], F32R) for q in range(2)]
        w_lo = [sb(f"w{q}_lo", [P, OPS, OPW], F32R) for q in range(2)]
        ident = sb("ident", [P, P])
        meta_next = sb("meta_next", [P, E])
        meta_now = sb("meta_now", [P, E])
        token_next = sb("token_next", [P, 1], I32)
        token_now = sb("token_now", [P, 1], I32)
        token_out = sb("token_out", [P, 1], I32)
        y_row = sb("y_row", [P, 1], I32)
        no_shift = sb("no_shift", [P, 1], I32)
        early_blocks = sb("early_blocks", [P, 1], I32)
        arrived = sb("arrived", [P, 1], I32)
        table = sb("table", [1, 5 * E], I32)
        pad = sb("pad", [P, ROW])

        part1 = ExitStack()
        S = sb("S", [P, TILES, N], F32, part1)
        work = sb("work", [P, 4096 + TB * ROW + 2 * D], F32, part1)
        xb_own = sb("xb_own", [P, XBUFS - 1, TB, D], F32, part1)
        rows_own = sb("rows_own", [P, TB, ROW], F32, part1)
        wq = sb("wq", [P, P], F32, part1)
        wk = sb("wk", [P, P], F32, part1)
        gate_w = sb("gate_w", [P, DC, E], F32, part1)
        upper = sb("upper", [P, P], BF16, part1)
        ones_b = sb("ones_b", [P, P], BF16, part1)
        ones_f = sb("ones_f", [P, 1], F32, part1)
        gain_in = sb("gain_in", [P, 3], F32, part1)
        gain = sb("gain", [P, 6], F32, part1)
        tanh_x, gamma, tanh_f, c1, c2, neg_c1 = (gain[:, k:k + 1] for k in range(6))
        small = sb("small", [P, 16], F32, part1)
        sim_stats = sb("sim_stats", [P, B, TB, 6], F32, part1)
        sim_mv = sb("sim_mv", [P, TILES, 2], F32, part1)
        sim_sd = sb("sim_sd", [P, TILES], F32, part1)
        half_pow = sb("half_pow", [P, TILES], F32, part1)
        rsqrt_pow = sb("rsqrt_pow", [P, TB], F32, part1)
        low = sb("low", [P, TILES, 2], F32, part1)
        high = sb("high", [P, TILES, 2], F32, part1)
        probe = sb("probe", [P, TILES, 2], F32, part1)
        act_sum = sb("act_sum", [P, TILES], F32, part1)
        is_low = sb("is_low", [P, HALF, 2], I32, part1)
        is_high = sb("is_high", [P, HALF, 2], I32, part1)
        in_window = sb("in_window", [P, TILES], I32, part1)
        span = sb("span", [P, HALF, 2], F32, part1)
        frac = sb("frac", [P, HALF], F32, part1)
        inv = sb("inv", [P, HALF], F32, part1)
        count = sb("count", [P, TILES], F32, part1)
        top8 = sb("top8", [P, TILES, 8], F32, part1)
        rank8 = sb("rank8", [P, TILES, 8], F32, part1)
        pick = sb("pick", [P, TILES, 8], F32, part1)
        thr = sb("thr", [P, TILES], F32, part1)
        settled = sb("settled", [P, 1], F32, part1)
        settled_i = sb("settled_i", [P, 1], I32, part1)
        max8 = sb("max8", [P, 8], F32, part1)
        ln_stats = sb("ln_stats", [P, TB, 6], F32, part1)
        ln_mv = sb("ln_mv", [P, 2, B, TB, 2], F32, part1)
        ln_v = sb("ln_v", [P, 2, B, TB], F32, part1)
        ln_r = sb("ln_r", [P, 2, B, TB], F32, part1)
        ln_m = sb("ln_m", [P, 2, B, TB], F32, part1)
        ln_s = sb("ln_s", [P, B, TB], F32, part1)
        ln_o = sb("ln_o", [P, 2, B, TB], F32, part1)
        score = sb("score", [P, TB, E], F32, part1)
        best = sb("best", [P, TB, 8], F32, part1)
        best_at = sb("best_at", [P, TB, 8], U32, part1)
        best_f = sb("best_f", [P, TB, 2], F32, part1)
        lead = sb("lead", [P, TB, 2], F32, part1)
        share = sb("share", [P, TB, 2], F32, part1)
        expert_no = sb("expert_no", [P, TB, 2, E], F32, part1)
        chosen = sb("chosen", [P, TB, 2, E], F32, part1)
        weighed = sb("weighed", [P, TB, 2, E], F32, part1)
        mask = sb("mask", [P, TB, E], BF16, part1)
        before = sb("before", [P, B + 1, E], BF16, part1)
        mask_sum = sb("mask_sum", [P, E], F32, part1)
        region_row = sb("region_row", [P, TB, E], F32, part1)
        place = sb("place", [P, TB, E], F32, part1)
        place_of = sb("place_of", [P, TB, 2, E], F32, part1)
        place_f = sb("place_f", [P, TB, 2], F32, part1)
        place_i = sb("place_i", [P, B, TB, 2], I32, part1)
        token_no = sb("token_no", [P, TILES], I32, part1)
        early_i = sb("early_i", [P, 1], I32, part1)
        blk_i = sb("blk_i", [P, E], I32, part1)
        blk_j = sb("blk_j", [P, E], I32, part1)
        blk_f = sb("blk_f", [P, E], F32, part1)
        blk_1 = sb("blk_1", [P, E], F32, part1)
        table_f = sb("table_f", [P, 5 * E], F32, part1)
        part1.close()

        xtile = sb("xtile", [P, ROW])
        xT_hi = sb("xT_hi", [P, DC, P], F32R)
        xT_lo = sb("xT_lo", [P, DC, P], F32R)
        hT_hi = sb("hT_hi", [P, 2, COLS], F32R)
        hT_lo = sb("hT_lo", [P, 2, COLS], F32R)
        act_g = sb("act_g", [P, 2, COLS])
        h = sb("h", [P, 2, COLS])
        y = sb("y", [P, D])
        w_hi.append(sb("w2_hi", [P, OPS, OPW], F32R))
        w_lo.append(sb("w2_lo", [P, OPS, OPW], F32R))

        ctx_sb = work[:, 0:2048].rearrange("p (b n) -> p b n", b=B)
        QT, KT = ([work[:, first + 512 * k:first + 512 * (k + 1)] for k in range(2)] for first in (3072, 4096))
        flags = [work[:, 3072 + 256 * k:3328 + 256 * k].bitcast(BF16) for k in range(ON_VECTOR)]
        signs = [work[:, 3840 + 128 * k:3968 + 128 * k].bitcast(I8) for k in range(2 * (HALF - ON_VECTOR))]
        IN_WORK = (4096 + TB * ROW + 2 * D) // N
        masked = [work[:, N * k:N * (k + 1)] for k in range(IN_WORK)]
        masked += [rows_own[:, :, :].rearrange("p i n -> p (i n)")[:, N * k:N * (k + 1)] for k in range(TILES - IN_WORK)]
        below = [raw[:, 2, TB * D + 128 * k:TB * D + 128 * (k + 1)].bitcast(I8) for k in range(TILES)]
        left_over = masked[TILES - 1]
        A = [work[:, 2048 * k:2048 * (k + 1)].rearrange("p (i n) -> p i n", i=TB) for k in range(2)]
        rows = [rows_own, work[:, 4096:4096 + TB * ROW].rearrange("p (i n) -> p i n", i=TB),
                S[:, :, :].rearrange("p t n -> p (t n)")[:, TILES * N - TB * ROW:].rearrange("p (i n) -> p i n", i=TB), rows_own]
        xfT = [work[:, 4096 + TB * ROW + D * k:4096 + TB * ROW + D * (k + 1)] for k in range(2)]
        xb = [xb_own[:, k, :, :] for k in range(XBUFS - 1)] + [raw[:, 2, 0:TB * D].rearrange("p (i n) -> p i n", i=TB)]

        bank = [stack.enter_context(nc.psum_tensor(f"bank{k}", [P, COLS], F32)) for k in range(8)]
        GATE, UP, Y_BANK, X_BANK = (0, 2), (1, 3), 7, 6
        H_BANK = (4, 5)
        scores_ps = bank[6][:, 0:TB * E].rearrange("p (i e) -> p i e", e=E)
        rank_ps = bank[7][:, 0:TB * E].rearrange("p (i e) -> p i e", e=E)
        early_ps = bank[7][:, TB * E:TB * E + 1]
        total_ps = bank[0][:, 0:E]
        settled_ps = bank[6][0:1, 64:65]

        wqk_in, gate_in, gain_in_s = sem("wqk_in"), sem("gate_in"), sem("gain_in_s")
        ctx_in = [sem(f"ctx_in{b}") for b in range(B)]
        x_in = [sem(f"x_in{k}") for k in range(XBUFS)]
        raw_in = [sem(f"raw_in{q}") for q in range(GROUPS)]
        raw_in_0 = [sem(f"raw_in_0_{q}") for q in range(GROUPS)]
        consts = sem("consts")
        qk_mm, qk_out, sim_mm, sim_out = sem("qk_mm"), sem("qk_out"), sem("sim_mm"), sem("sim_out")
        sim_moments, sd_set = sem("sim_moments"), sem("sd_set")
        probe_set = [sem("probe_set0"), sem("probe_set1")]
        act_counted = [sem("act_counted0"), sem("act_counted1")]
        probe_final, flagged, masked_own, masked_pool = sem("probe_final"), sem("flagged"), sem("masked_own"), sem("masked_pool")
        top8_set, all_counted = sem("top8_set"), sem("all_counted")
        settled_set, settled_mm, thr_set = sem("settled_set"), sem("settled_mm"), sem("thr_set")
        gains_act, gains_set = sem("gains_act"), sem("gains_set")
        ln1_stats, ln2_stats, base_set = sem("ln1_stats"), sem("ln2_stats"), sem("base_set")
        ln1_set, ln2_set, pads_in = sem("ln1_set"), sem("ln2_set"), sem("pads_in")
        sig_set, A_set, AA_mm, x1_set = sem("sig_set"), sem("A_set"), sem("AA_mm"), sem("x1_set")
        x1_stored = [sem(f"x1_stored{k}") for k in range(XBUFS)]
        rows_set, xfT_mm, xfT_out, scores_mm = sem("rows_set"), sem("xfT_mm"), sem("xfT_out"), sem("scores_mm")
        lead_set, share_set, mask_set, rank_mm = sem("lead_set"), sem("share_set"), sem("mask_set"), sem("rank_mm")
        place_set, routed_in, total_mm = sem("place_set"), [sem(f"routed_in{b}") for b in range(B)], sem("total_mm")
        early_set, first_pads_in = sem("early_set"), sem("first_pads_in")
        table_set, pool_step = sem("table_set"), sem("pool_step")
        hi_set = [sem(f"hi_set{q}") for q in range(GROUPS)]
        lo_set = [sem(f"lo_set{q}") for q in range(GROUPS)]
        xtile_free, y_out = sem("xtile_free"), sem("y_out")
        xtile_in, xT_mm, xhi_set, xT_set = sem("xtile_in"), sem("xT_mm"), sem("xhi_set"), sem("xT_set")
        gate_mm, up_mm = [sem("gate_mm0"), sem("gate_mm1")], [sem("up_mm0"), sem("up_mm1")]
        silu_set, h_set = [sem("silu_set0"), sem("silu_set1")], [sem("h_set0"), sem("h_set1")]
        hT_mm, hhi_set = [sem("hT_mm0"), sem("hT_mm1")], [sem("hhi_set0"), sem("hhi_set1")]
        hT_set = [sem("hT_set0"), sem("hT_set1")]
        y_mm, y_set, y_added = sem("y_mm"), sem("y_set"), sem("y_added")

        def entry(eng, row, e, least, most):
            return eng.value_load(table[0:1, bass.ds(e + row * E, 1)], min_val=least, max_val=most)

        def blocks(eng, e):
            first = entry(eng, 0, e, 0, MOST_BLOCKS - 1)
            end = entry(eng, 1, e, 1, MOST_BLOCKS)
            return eng.Fori(first, end)

        block = stack.enter_context(nc.Block())

        @block.sync
        def _(sp):
            sp.dma_start(wq[:, :], wqT).then_inc(wqk_in, 16)
            sp.dma_start(wk[:, :], wkT).then_inc(wqk_in, 16)
            for b in range(B):
                sp.dma_start(ctx_sb[:, b, :], ctxT[:, b, :]).then_inc(ctx_in[b], 16)
            for b in range(XBUFS):
                sp.dma_start(xb[b][:, :, :], x_tiles[b]).then_inc(x_in[b], 16)
            sp.dma_start(gate_w[:, :, :], gateT).then_inc(gate_in, 16)
            for q in range(2):
                sp.dma_start(raw[:, q, :], w_groups[0, q]).then_inc(raw_in_0[q], 16)
            for b in range(B):
                k = b % XBUFS
                sp.wait_ge(x1_set, TB * (b + 1))
                sp.dma_start(out_tiles[b], xb[k][:, :, :]).then_inc(x1_stored[k], 16)
                if b + XBUFS < B:
                    sp.wait_ge(x1_stored[k], 16)
                    sp.wait_ge(rows_set, TB * (b + 1))
                    sp.dma_start(xb[k][:, :, :], x_tiles[b + XBUFS]).then_inc(x_in[k], 16)
            sp.wait_ge(early_set, 1)
            early = sp.value_load(early_blocks[0:1, 0:1], min_val=0, max_val=TOKENS // P)
            for b in range(SOON):
                sp.wait_ge(routed_in[b], 16 * 2 * TB)

            def fill_up(e, done):
                at = entry(sp, 4, e, 0, E * REGION - P)
                sp.dma_start(routed[bass.ds(at, P), :], pad[:, :]).then_inc(done, 16)

            with sp.If(early < 1):
                sp.wait_ge(table_set, 1)
                fill_up(0, first_pads_in)
                sp.wait_ge(first_pads_in, 16)
                for b in range(SOON, B):
                    sp.wait_ge(routed_in[b], 16 * 2 * TB)
            with sp.Else():
                sp.nop()
            sp.dma_start(xtile[:, :], routed[0:P, :]).then_inc(xtile_in, 16)
            sp.wait_ge(x1_stored[XBUFS - 1], 16)
            sp.wait_ge(rows_set, TB * XBUFS)
            sp.dma_start(raw[:, 2, :], w_groups[0, 2]).then_inc(raw_in_0[2], 16)
            sp.wait_ge(table_set, 1)
            sp.wait_ge(xtile_in, 16)
            with sp.Fori(0, E) as e:
                fill_up(e, pads_in)
                first = entry(sp, 0, e, 0, MOST_BLOCKS - 1)
                some = entry(sp, 3, e, 1, REGION // P)
                with sp.Fori(0, some) as j:
                    with sp.If(first + j >= 1):
                        sp.wait_ge(pads_in, e * 16 + 16)
                        for b in range(SOON, B):
                            sp.wait_ge(routed_in[b], 16 * 2 * TB)
                        sp.wait_ge(xtile_free, first + j)
                        sp.dma_start(xtile[:, :], routed[bass.ds(e * REGION + j * P, P), :]).then_inc(xtile_in, 16)
                    with sp.Else():
                        sp.nop()
            end = sp.value_load(table[0:1, 2 * E - 1:2 * E], min_val=1, max_val=MOST_BLOCKS)
            sp.wait_ge(xtile_free, end)
            sp.dma_start(xtile[:, :], routed[0:P, :]).then_inc(xtile_in, 16)

        @block.gpsimd
        def _(pool):
            nc.gpsimd.memset(half_pow[:, :], 0.5)
            nc.gpsimd.memset(rsqrt_pow[:, :], -0.5)
            nc.gpsimd.memset(ident[:, :], 0.0)
            nc.gpsimd.memset(no_shift[:, :], 0)
            nc.gpsimd.memset(upper[:, :], 1.0)
            nc.gpsimd.memset(ones_b[:, :], 1.0)
            nc.gpsimd.memset(ones_f[:, :], 1.0)
            nc.gpsimd.memset(pad[:, :], 0.0)
            nc.gpsimd.memset(before[:, 0, :], 0.0)
            nc.gpsimd.iota(rank8[:, :, :], [[0, TILES], [1, 8]], 1, 0, allow_small_or_imprecise_dtypes=True)
            nc.gpsimd.iota(expert_no[:, :, :, :], [[0, 2 * TB], [1, E]], 0, 0, allow_small_or_imprecise_dtypes=True)
            nc.gpsimd.iota(region_row[:, :, :], [[0, TB], [REGION, E]], 0, 0, allow_small_or_imprecise_dtypes=True)
            nc.gpsimd.iota(token_no[:, :], [[P, TILES]], 0, 1)
            pool.drain()
            nc.gpsimd.affine_select(out=ident[:, :], in_=ident[:, :], compare_op=ALU.not_equal, fill=1.0,
                                    base=0, pattern=[[-1, P]], channel_multiplier=1)
            nc.gpsimd.affine_select(out=upper[:, :], in_=upper[:, :], compare_op=ALU.is_gt, fill=0.0,
                                    base=0, pattern=[[1, P]], channel_multiplier=-1)
            nc.gpsimd.iota(pad[:, ROW - 1:ROW].bitcast(I32), [[0, 1]], TOKENS, 1)
            pool.drain()
            nc.gpsimd.memset(small[:, 0:1], 0.0).then_inc(consts, 1)
            pool.wait_ge(consts, 1)
            pool.dma_start(out[TOKENS:TOKENS + P, :], pad[:, 0:D]).then_inc(y_added, 16)

            for half in range(2):
                ts = slice(half * HALF, (half + 1) * HALF)
                pool.wait_ge(sim_moments, half + 1)
                nc.gpsimd.tensor_tensor(sim_sd[:, ts], sim_mv[:, ts, 1], half_pow[:, ts], ALU.pow).then_inc(sd_set, 1)

            steps = [0]

            def then(instruction):
                steps[0] += 1
                instruction.then_inc(pool_step, 1)
                pool.wait_ge(pool_step, steps[0])

            def scales(k, b, stats, done):
                pool.wait_ge(stats, b + 1)
                then(nc.gpsimd.tensor_scalar(ln_v[:, k, b, :], ln_mv[:, k, b, :, 1], EPS, 1.0, ALU.add, ALU.mult))
                then(nc.gpsimd.tensor_tensor(ln_r[:, k, b, :], ln_v[:, k, b, :], rsqrt_pow[:, :], ALU.pow))
                then(nc.gpsimd.tensor_tensor(ln_m[:, k, b, :], ln_r[:, k, b, :], ln_mv[:, k, b, :, 0], ALU.mult))
                if k == 0:
                    nc.gpsimd.tensor_scalar(ln_s[:, b, :], ln_r[:, k, b, :], c1, 1.0, ALU.mult, ALU.add)
                nc.gpsimd.tensor_scalar(ln_o[:, k, b, :], ln_m[:, k, b, :], neg_c1 if k == 0 else -1.0, 1.0,
                                        ALU.mult, ALU.mult).then_inc(done, 1)

            def route(b, tiles):
                pool.wait_ge(place_set, b + 1)
                for i in tiles:
                    for k in range(2):
                        nc.gpsimd.indirect_dma_start(
                            routed, bass.IndirectOffsetOnAxis(ap=place_i[:, b, i, k:k + 1], axis=0),
                            rows[b][:, i, :], None, bounds_check=E * REGION - 1, oob_is_err=True,
                        ).then_inc(routed_in[b], 16)

            pool.wait_ge(gains_set, 1)
            for b in range(EARLY):
                scales(0, b, ln1_stats, ln1_set)
                pool.drain()
                for i in range(TB):
                    nc.gpsimd.tensor_scalar(xb[b][:, i, :], xb[b][:, i, :], ln_s[:, b, i:i + 1],
                                            ln_o[:, 0, b, i:i + 1], ALU.mult, ALU.add).then_inc(base_set, 1)
            for t in range(ON_POOL):
                pool.wait_ge(flagged, t + 1)
                nc.gpsimd.tensor_tensor(masked[t], masked[t], S[:, t, :], ALU.add).then_inc(masked_pool, 1)
            for q in range(2):
                for j in range(OPS):
                    pool.wait_ge(hi_set[q], j + 1)
                    nc.gpsimd.tensor_tensor(w_lo[q][:, j, :], raw[:, q, j * OPW:(j + 1) * OPW], w_hi[q][:, j, :].bitcast(F32),
                                            ALU.subtract).then_inc(lo_set[q], 1)
            scales(0, 2, ln1_stats, ln1_set)
            scales(1, 0, ln2_stats, ln2_set)
            scales(1, 1, ln2_stats, ln2_set)
            route(0, range(TB))
            scales(0, 3, ln1_stats, ln1_set)
            scales(1, 2, ln2_stats, ln2_set)
            route(1, range(TB // 2))
            scales(1, 3, ln2_stats, ln2_set)
            route(1, range(TB // 2, TB))
            route(2, range(TB))
            route(3, range(TB))

            pool.wait_ge(xT_set, 2)
            pool.wait_ge(table_set, 1)
            pool.wait_ge(y_added, 16)
            for k in range(XBUFS):
                pool.wait_ge(x1_stored[k], 16 * len(range(k, B, XBUFS)))

            def add_blocks(e):
                with blocks(pool, e) as g:
                    pool.wait_ge(y_set, g + 1)
                    nc.gpsimd.tensor_tensor(y_row[:, :], token_out[:, :], no_shift[:, :], ALU.add)
                    pool.drain()
                    nc.gpsimd.indirect_dma_start(
                        out, bass.IndirectOffsetOnAxis(ap=y_row[:, 0:1], axis=0), y[:, :], None,
                        bounds_check=TOKENS + P - 1, oob_is_err=True, compute_op=ALU.add,
                    ).then_inc(y_added, 16)

            def split_w2(e):
                pool.wait_ge(raw_in[2], e * 16 + 16)
                nc.gpsimd.tensor_tensor(arrived[:, :], no_shift[:, :], no_shift[:, :], ALU.add)
                for j in range(OPS):
                    if j >= W2_BY_ACT:
                        nc.gpsimd.tensor_scalar(w_hi[2][:, j, :], raw[:, 2, j * OPW:(j + 1) * OPW], 1.0, 1.0,
                                                ALU.mult, ALU.mult).then_inc(hi_set[2], 1)
                    pool.wait_ge(hi_set[2], e * OPS + OPS + j + 1)
                    nc.gpsimd.tensor_tensor(w_lo[2][:, j, :], raw[:, 2, j * OPW:(j + 1) * OPW], w_hi[2][:, j, :].bitcast(F32),
                                            ALU.subtract).then_inc(lo_set[2], 1)

            with pool.Fori(0, E - 1) as e:
                for q in range(GROUPS):
                    pool.wait_ge(lo_set[q], OPS * e + OPS)
                    pool.dma_start(raw[:, q, :], w_groups[bass.ds(e + 1, 1), q, :, :].squeeze(0)).then_inc(raw_in[q], 16)
                add_blocks(e)
                split_w2(e)
            add_blocks(E - 1)
            end = pool.value_load(table[0:1, 2 * E - 1:2 * E], min_val=1, max_val=MOST_BLOCKS)
            pool.wait_ge(y_added, end * 16 + 16)

        @block.tensor
        def _(pe):
            pe.wait_ge(wqk_in, 32)

            def project(b):
                pe.wait_ge(ctx_in[b], 16)
                nc.tensor.matmul(bank[4 + b % 2 * 2][:, :], wq[:, :], ctx_sb[:, b, :], start=True, stop=True)
                nc.tensor.matmul(bank[5 + b % 2 * 2][:, :], wk[:, :], ctx_sb[:, b, :], start=True, stop=True).then_inc(qk_mm, 1)

            project(0)
            project(1)
            for b in range(B):
                pe.wait_ge(qk_out, b + 1)
                for i in range(TB):
                    if b > 0:
                        pe.wait_ge(sim_out, TB * (b - 1) + i + 1)
                    nc.tensor.matmul(bank[i][:, :], QT[b % 2][:, i * P:(i + 1) * P], KT[b % 2], start=True, stop=True).then_inc(sim_mm, 1)
                if b + 2 < B:
                    project(b + 2)
            pe.wait_ge(settled_set, 1)
            pe.wait_ge(consts, 1)
            nc.tensor.matmul(settled_ps, ones_f[:, :], settled[:, :], start=True, stop=True).then_inc(settled_mm, 1)

            def add_transposed(b, tiles):
                At = A[b % 2]
                pe.wait_ge(A_set, b + 1)
                for i in tiles:
                    if b > 0:
                        pe.wait_ge(x1_set, TB * (b - 1) + i + 1)
                    nc.tensor.matmul(bank[i][:, :], ident[:, :], At[:, i, :], start=True, stop=False)
                    for j in range(TB):
                        last = nc.tensor.matmul(bank[i][:, j * P:(j + 1) * P], At[:, j, i * P:(i + 1) * P],
                                                ident[:, :], start=False, stop=(j == TB - 1))
                    last.then_inc(AA_mm, 1)

            def scores(b):
                if b == 0:
                    pe.wait_ge(gate_in, 16)

                def transpose_tile(i):
                    pe.wait_ge(rows_set, TB * b + i + 1)
                    if TB * b + i >= 2:
                        pe.wait_ge(xfT_out, TB * b + i - 1)
                    for c in range(DC):
                        last = nc.tensor.transpose(bank[4 + i % 2][:, c * P:(c + 1) * P], rows[b][:, i, c * P:(c + 1) * P], ident[:, :])
                    last.then_inc(xfT_mm, 1)

                transpose_tile(0)
                for i in range(TB):
                    if i + 1 < TB:
                        transpose_tile(i + 1)
                    pe.wait_ge(xfT_out, TB * b + i + 1)
                    for c in range(DC):
                        last = nc.tensor.matmul(scores_ps[:, i, :], xfT[i % 2][:, c * P:(c + 1) * P], gate_w[:, c, :],
                                                start=(c == 0), stop=(c == DC - 1))
                    last.then_inc(scores_mm, 1)

            def ranks(b):
                pe.wait_ge(mask_set, b + 1)
                for i in range(TB):
                    nc.tensor.matmul(rank_ps[:, i, :], upper[:, :], mask[:, i, :], start=True, stop=False)
                    for j in range(i):
                        nc.tensor.matmul(rank_ps[:, i, :], ones_b[:, :], mask[:, j, :], start=False, stop=False)
                    last = nc.tensor.matmul(rank_ps[:, i, :], ones_b[:, :], before[:, b, :], start=False, stop=True)
                if b == SOON - 1:
                    last = nc.tensor.matmul(early_ps, ones_b[:, :], before[:, b + 1, 0:1], start=True, stop=True)
                last.then_inc(rank_mm, 1)

            add_transposed(0, range(TB))
            add_transposed(1, range(TB))
            scores(0)
            for b in range(1, B):
                if b + 1 < B:
                    add_transposed(b + 1, range(TB // 2))
                ranks(b - 1)
                if b + 1 < B:
                    add_transposed(b + 1, range(TB // 2, TB))
                scores(b)
            pe.wait_ge(mask_set, B)
            nc.tensor.matmul(total_ps, ones_b[:, :], before[:, B, :], start=True, stop=True).then_inc(total_mm, 1)
            ranks(B - 1)

            def three(out_ap, hi, lo, hi_w, lo_w, start, stop):
                nc.tensor.matmul(out_ap, hi, hi_w, start=start, stop=False)
                nc.tensor.matmul(out_ap, lo, hi_w, start=False, stop=False)
                return nc.tensor.matmul(out_ap, hi, lo_w, start=False, stop=stop)

            def transpose_x(n):
                pe.wait_ge(xtile_in, n * 16)
                for c in range(DC):
                    last = nc.tensor.transpose(bank[X_BANK][:, c * P:(c + 1) * P], xtile[:, c * P:(c + 1) * P], ident[:, :])
                last.then_inc(xT_mm, 1)

            def first_layer(s, which, c):
                into = (GATE if which == 0 else UP)[s]
                cols = slice(which * COLS, (which + 1) * COLS)
                last = three(bank[into][:, :], xT_hi[:, c, :], xT_lo[:, c, :], w_hi[s][:, c, cols], w_lo[s][:, c, cols],
                             c == 0, c == DC - 1)
                if c == DC - 1:
                    last.then_inc((gate_mm if which == 0 else up_mm)[s], 1)

            def transpose_h(s):
                for c in range(DC):
                    last = nc.tensor.transpose(bank[H_BANK[s]][:, c * P:(c + 1) * P], h[:, s, c * P:(c + 1) * P], ident[:, :])
                last.then_inc(hT_mm[s], 1)

            def second_layer(chunks):
                for k in chunks:
                    s, cols = k // DC, slice(k % DC * P, (k % DC + 1) * P)
                    w_cols = slice(k % 2 * COLS, (k % 2 + 1) * COLS)
                    last = three(bank[Y_BANK][:, :], hT_hi[:, s, cols], hT_lo[:, s, cols], w_hi[2][:, k // 2, w_cols],
                                 w_lo[2][:, k // 2, w_cols], k == 0, k == IC - 1)
                return last

            transpose_x(1)
            pe.wait_ge(table_set, 1)
            with pe.Fori(0, E) as e:
                split = [pe.snap(e * OPS + j + 1) for j in range(OPS)]
                with blocks(pe, e) as g:
                    nth = pe.snap(g + 1)
                    pe.wait_ge(xT_set, nth)
                    for c in range(DC):
                        pe.wait_ge(lo_set[0], split[c])
                        first_layer(0, 0, c)
                        first_layer(0, 1, c)
                    for c in range(2):
                        pe.wait_ge(lo_set[1], split[c])
                        first_layer(1, 0, c)
                        first_layer(1, 1, c)
                    for c in range(2, DC):
                        pe.wait_ge(lo_set[1], split[c])
                        first_layer(1, 0, c)
                    pe.wait_ge(h_set[0], nth)
                    transpose_h(0)
                    for c in range(2, DC):
                        first_layer(1, 1, c)
                    transpose_x(nth + 1)
                    pe.wait_ge(hT_set[0], nth)
                    pe.wait_ge(lo_set[2], split[0])
                    pe.wait_ge(y_out, nth)
                    second_layer([0])
                    pe.wait_ge(h_set[1], nth)
                    transpose_h(1)
                    second_layer([1])
                    pe.wait_ge(lo_set[2], split[1])
                    second_layer([2, 3])
                    pe.wait_ge(hT_set[1], nth)
                    pe.wait_ge(lo_set[2], split[2])
                    second_layer([4, 5])
                    pe.wait_ge(lo_set[2], split[3])
                    second_layer([6, 7]).then_inc(y_mm, 1)

        @block.scalar
        def _(act):
            act.dma_start(gain_in[:, :], gains.partition_broadcast(P)).then_inc(gain_in_s, 16)
            nc.scalar.preload_act_table(ACT.Sigmoid)
            act.wait_ge(gain_in_s, 16)
            nc.scalar.activation(tanh_x, gain_in[:, 0:1], ACT.Tanh)
            nc.scalar.activation(gamma, gain_in[:, 1:2], ACT.Sigmoid)
            nc.scalar.activation(tanh_f, gain_in[:, 2:3], ACT.Tanh).then_inc(gains_act, 1)

            def projected(b):
                act.wait_ge(qk_mm, b + 1)
                if b >= 2:
                    act.wait_ge(sim_mm, TB * (b - 1))
                nc.scalar.activation(QT[b % 2], bank[4 + b % 2 * 2][:, :], ACT.Copy)
                nc.scalar.activation(KT[b % 2], bank[5 + b % 2 * 2][:, :], ACT.Copy).then_inc(qk_out, 1)

            projected(0)
            projected(1)
            for b in range(B):
                for i in range(TB):
                    act.wait_ge(sim_mm, b * TB + i + 1)
                    nc.scalar.activation(S[:, b * TB + i, :], bank[i][:, :], ACT.Copy).then_inc(sim_out, 1)
                if b + 2 < B:
                    projected(b + 2)
            with act.Fori(0, SEARCH) as k:
                for half in range(2):
                    act.wait_ge(probe_set[half], k + 1)
                    for n in range(ON_VECTOR, HALF):
                        t = half * HALF + n
                        last = nc.scalar.activation(signs[half * (HALF - ON_VECTOR) + n - ON_VECTOR], S[:, t, :], ACT.Sign, bias=probe[:, t, 0:1], scale=-1.0,
                                                    accum_out=act_sum[:, t:t + 1])
                    last.then_inc(act_counted[half], 1)

            def count_masked(t):
                return nc.scalar.activation(below[t], masked[t], ACT.Sign, bias=small[:, 6:7], scale=1.0,
                                            accum_out=act_sum[:, t:t + 1])

            def split_high(q, steps):
                for j in steps:
                    nc.scalar.activation(w_hi[q][:, j, :], raw[:, q, j * OPW:(j + 1) * OPW], ACT.Copy).then_inc(hi_set[q], 1)

            act.wait_ge(raw_in_0[0], 16)
            split_high(0, range(OPS))
            act.wait_ge(probe_final, 1)
            for t in range(ON_POOL // 2):
                act.wait_ge(masked_pool, t + 1)
                count_masked(t)
            for t in range(ON_POOL, TILES):
                act.wait_ge(masked_own, t - ON_POOL + 1)
                count_masked(t)
            for t in range(ON_POOL // 2, ON_POOL):
                act.wait_ge(masked_pool, t + 1)
                last = count_masked(t)
            last.then_inc(all_counted, 1)

            def sigmoids(b):
                if b >= 2:
                    act.wait_ge(AA_mm, TB * (b - 1))
                act.wait_ge(top8_set, TILES // 2)
                act.wait_ge(all_counted, 1)
                nc.scalar.activation(A[b % 2], S[:, b * TB:(b + 1) * TB, :], ACT.Sigmoid, scale=SIM_SCALE).then_inc(sig_set, 1)

            def xfT_copies(b):
                for i in range(TB):
                    act.wait_ge(xfT_mm, TB * b + i + 1)
                    if TB * b + i >= 2:
                        act.wait_ge(scores_mm, TB * b + i - 1)
                    nc.scalar.activation(xfT[i % 2], bank[4 + i % 2][:, :], ACT.Copy).then_inc(xfT_out, 1)

            def normal_rows(b):
                act.wait_ge(ln2_set, b + 1)
                if b < 2:
                    act.wait_ge(thr_set, 1)
                if b == 2:
                    act.wait_ge(A_set, B)
                if b == 3:
                    act.wait_ge(routed_in[0], 16 * 2 * TB)
                for i in range(TB):
                    nc.scalar.activation(rows[b][:, i, 0:D], xb[b % XBUFS][:, i, :], ACT.Identity, bias=ln_o[:, 1, b, i:i + 1],
                                         scale=ln_r[:, 1, b, i:i + 1]).then_inc(rows_set, 1)

            def late_base(b):
                act.wait_ge(ln1_set, b + 1)
                for i in range(TB):
                    nc.scalar.activation(xb[b % XBUFS][:, i, :], xb[b % XBUFS][:, i, :], ACT.Identity,
                                         bias=ln_o[:, 0, b, i:i + 1], scale=ln_s[:, b, i:i + 1]).then_inc(base_set, 1)

            def shares(b):
                act.wait_ge(lead_set, b + 1)
                nc.scalar.activation(share[:, :, :], lead[:, :, :], ACT.Sigmoid).then_inc(share_set, 1)

            sigmoids(0)
            sigmoids(1)
            act.wait_ge(raw_in_0[1], 16)
            split_high(1, range(OPS))
            sigmoids(2)
            normal_rows(0)
            xfT_copies(0)
            for b in range(1, B):
                if b + 2 < B:
                    sigmoids(b + 2)
                shares(b - 1)
                normal_rows(b)
                xfT_copies(b)
                if b == 1:
                    late_base(2)
                    late_base(3)
            shares(B - 1)

            nc.scalar.preload_act_table(ACT.Silu)
            act.wait_ge(total_mm, 1)

            def x_high(n):
                act.wait_ge(xT_mm, n)
                nc.scalar.activation(xT_hi[:, :, :], bank[X_BANK][:, :].rearrange("p (c n) -> p c n", c=DC), ACT.Copy).then_inc(xhi_set, 1)

            def silu(s, nth):
                act.wait_ge(gate_mm[s], nth)
                nc.scalar.activation(act_g[:, s, :], bank[GATE[s]][:, :], ACT.Silu).then_inc(silu_set[s], 1)

            def h_high(s, nth):
                act.wait_ge(hT_mm[s], nth)
                nc.scalar.activation(hT_hi[:, s, :], bank[H_BANK[s]][:, :], ACT.Copy).then_inc(hhi_set[s], 1)

            x_high(1)
            for b in (1, 2):
                act.wait_ge(routed_in[b], 16 * 2 * TB)
            act.wait_ge(raw_in_0[2], 16)
            split_high(2, range(OPS))
            act.wait_ge(table_set, 1)
            with act.Fori(0, E) as e:
                change = entry(act, 2, e, 0, 1 << 20)
                arrived = act.snap(e * 16 + 16)
                with blocks(act, e) as g:
                    nth = act.snap(g + 1)
                    silu(0, nth)
                    silu(1, nth)
                    h_high(0, nth)
                    x_high(nth + 1)
                    h_high(1, nth)
                    with act.If(g == change):
                        act.wait_ge(up_mm[0], nth)
                        act.wait_ge(raw_in[0], arrived)
                        split_high(0, range(OPS))
                        act.wait_ge(up_mm[1], nth)
                        act.wait_ge(raw_in[1], arrived)
                        split_high(1, range(OPS))
                        act.wait_ge(y_mm, nth)
                        act.wait_ge(raw_in[2], arrived)
                        split_high(2, range(W2_BY_ACT))
                    with act.Else():
                        act.nop()
                    act.nop()

        @block.vector
        def _(dve):
            V = nc.vector

            def stats(k, b, done):
                for i in range(TB):
                    V.bn_stats(ln_stats[:, i, :], xb[b % XBUFS][:, i, :])
                dve.drain()
                for i in range(TB):
                    last = V.bn_aggr(ln_mv[:, k, b, i, :], ln_stats[:, i, :])
                last.then_inc(done, 1)
                dve.drain()

            def x_stats(b):
                dve.wait_ge(x_in[b % XBUFS], 16 * (b // XBUFS + 1))
                stats(0, b, ln1_stats)

            V.memset(low[:, :, 1], 360.0)
            V.memset(high[:, :, 1], 20.0)

            def first_probes(half):
                ts = slice(half * HALF, (half + 1) * HALF)
                dve.wait_ge(sd_set, half + 1)
                V.scalar_tensor_tensor(probe[:, ts, 0], sim_sd[:, ts], 0.5, sim_mv[:, ts, 0], ALU.mult, ALU.add).then_inc(probe_set[half], 1)
                V.scalar_tensor_tensor(low[:, ts, 0], sim_sd[:, ts], -0.66, sim_mv[:, ts, 0], ALU.mult, ALU.add)
                V.scalar_tensor_tensor(high[:, ts, 0], sim_sd[:, ts], 1.54, sim_mv[:, ts, 0], ALU.mult, ALU.add)

            for b in range(B):
                for i in range(TB):
                    dve.wait_ge(sim_out, TB * b + i + 1)
                    V.bn_stats(sim_stats[:, b, i, :], S[:, TB * b + i, :])
                if b % 2 == 1:
                    dve.drain()
                    for t in range(TB * (b - 1), TB * (b + 1)):
                        last = V.bn_aggr(sim_mv[:, t, :], sim_stats[:, t // TB, t % TB, :])
                    last.then_inc(sim_moments, 1)
                if b == 1:
                    x_stats(0)
                if b == 2:
                    first_probes(0)
            x_stats(1)
            first_probes(1)
            dve.wait_ge(gains_act, 1)
            V.tensor_tensor(small[:, 1:2], tanh_x, gamma, ALU.mult)
            dve.drain()
            V.tensor_tensor(c1, tanh_x, small[:, 1:2], ALU.subtract)
            V.tensor_scalar(c2, small[:, 1:2], 0.5, None, ALU.mult)
            dve.drain()
            V.tensor_scalar(neg_c1, c1, -1.0, None, ALU.mult).then_inc(gains_set, 1)

            with dve.Fori(0, SEARCH) as k:
                for half in range(2):
                    ts = slice(half * HALF, (half + 1) * HALF)
                    for n in range(ON_VECTOR):
                        t = half * HALF + n
                        V.tensor_scalar(flags[n], S[:, t, :], probe[:, t, 0:1], None, ALU.is_ge, ALU.add,
                                        accum_out=probe[:, t, 1:2])
                    dve.wait_ge(act_counted[half], k + 1)
                    at = slice(half * HALF + ON_VECTOR, (half + 1) * HALF)
                    V.tensor_scalar(probe[:, at, 1], act_sum[:, at], -0.5, N / 2.0, ALU.mult, ALU.add)
                    dve.drain()
                    counts = probe[:, ts, 1:2].to_broadcast([P, HALF, 2])
                    V.tensor_scalar(is_low[:, :, :], counts, float(KTH), None, ALU.is_ge)
                    V.tensor_scalar(is_high[:, :, :], counts, float(KTH), None, ALU.is_lt)
                    dve.drain()
                    V.copy_predicated(low[:, ts, :], is_low[:, :, :], probe[:, ts, :])
                    V.copy_predicated(high[:, ts, :], is_high[:, :, :], probe[:, ts, :])
                    dve.drain()
                    V.tensor_tensor(span[:, :, :], low[:, ts, :], high[:, ts, :], ALU.subtract)
                    dve.drain()
                    V.reciprocal(inv[:, :], span[:, :, 1])
                    dve.drain()
                    V.scalar_tensor_tensor(frac[:, :], low[:, ts, 1], -AIM, inv[:, :], ALU.add, ALU.mult)
                    dve.drain()
                    V.tensor_scalar(frac[:, :], frac[:, :], 0.05, 0.95, ALU.max, ALU.min)
                    dve.drain()
                    V.tensor_tensor(frac[:, :], frac[:, :], span[:, :, 0], ALU.mult)
                    dve.drain()
                    V.tensor_tensor(probe[:, ts, 0], low[:, ts, 0], frac[:, :], ALU.subtract).then_inc(probe_set[half], 1)
                    dve.drain()
            V.tensor_scalar(in_window[:, :], high[:, :, 1], float(KTH - WINDOW), None, ALU.is_ge)
            dve.drain()
            V.copy_predicated(probe[:, :, 0], in_window[:, :], high[:, :, 0])
            dve.drain()
            V.memset(small[:, 6:7], BIG / 4).then_inc(probe_final, 1)
            dve.drain()
            for t in range(TILES):
                V.tensor_scalar(masked[t], S[:, t, :], probe[:, t, 0:1], -BIG, ALU.is_ge, ALU.mult).then_inc(flagged, 1)
            dve.drain()
            for t in range(ON_POOL, TILES):
                V.tensor_tensor(masked[t], masked[t], S[:, t, :], ALU.add).then_inc(masked_own, 1)
            for t in range(TILES):
                if t < ON_POOL:
                    dve.wait_ge(masked_pool, t + 1)
                if t == ON_POOL:
                    dve.drain()
                V.max(top8[:, t, :], masked[t]).then_inc(top8_set, 1)
            dve.wait_ge(all_counted, 1)
            V.tensor_scalar(count[:, :], act_sum[:, :], 0.5, float(KTH) - N / 2.0, ALU.mult, ALU.add)
            dve.drain()
            V.tensor_tensor(pick[:, :, :], rank8[:, :, :], count[:, :].unsqueeze(2).to_broadcast([P, TILES, 8]), ALU.is_equal)
            dve.drain()
            V.tensor_reduce(settled[:, :], pick[:, :, :], AX.XY, ALU.add).then_inc(settled_set, 1)
            dve.drain()
            V.tensor_tensor(pick[:, :, :], pick[:, :, :], top8[:, :, :], ALU.mult)
            dve.drain()
            V.tensor_reduce(thr[:, :], pick[:, :, :], AX.X, ALU.add)
            dve.wait_ge(settled_mm, 1)
            V.tensor_copy(settled_i[0:1, :], settled_ps)
            dve.drain()
            rows_settled = dve.value_load(settled_i[0:1, 0:1], min_val=0, max_val=TOKENS)
            with dve.If(rows_settled < TOKENS):
                with dve.Fori(0, TILES) as t:
                    V.tensor_copy(left_over, S[:, bass.ds(t, 1), :].squeeze(1))
                    dve.drain()
                    with dve.Fori(0, (KTH - 1) // 8):
                        V.max(max8[:, :], left_over)
                        dve.drain()
                        V.match_replace(left_over, max8[:, :], left_over, -BIG)
                        dve.drain()
                    V.max(max8[:, :], left_over)
                    dve.drain()
                    r = (KTH - 1) % 8
                    V.tensor_copy(thr[:, bass.ds(t, 1)], max8[:, r:r + 1])
                    dve.drain()
            with dve.Else():
                dve.nop()
            V.memset(small[:, 3:4], 0.0).then_inc(thr_set, 1)
            dve.drain()

            def mask_A(b):
                dve.wait_ge(sig_set, b + 1)
                for i in range(TB):
                    t = b * TB + i
                    last = V.scalar_tensor_tensor(A[b % 2][:, i, :], S[:, t, :], thr[:, t:t + 1], A[b % 2][:, i, :],
                                                  ALU.is_ge, ALU.mult)
                last.then_inc(A_set, 1)

            def x1(b):
                for i in range(TB):
                    dve.wait_ge(AA_mm, TB * b + i + 1)
                    dve.wait_ge(base_set, TB * b + i + 1)
                    V.scalar_tensor_tensor(xb[b % XBUFS][:, i, :], bank[i][:, :], c2, xb[b % XBUFS][:, i, :],
                                           ALU.mult, ALU.add).then_inc(x1_set, 1)
                dve.drain()
                stats(1, b, ln2_stats)

            def choose(b):
                dve.wait_ge(scores_mm, TB * (b + 1))
                V.tensor_copy(score[:, :, :], scores_ps)
                dve.drain()
                for i in range(TB):
                    V.max(best[:, i, :], score[:, i, :])
                dve.drain()
                for i in range(TB):
                    V.max_index(best_at[:, i, :], best[:, i, :], score[:, i, :])
                V.tensor_tensor(lead[:, :, 0], best[:, :, 0], best[:, :, 1], ALU.subtract)
                V.tensor_tensor(lead[:, :, 1], best[:, :, 1], best[:, :, 0], ALU.subtract).then_inc(lead_set, 1)
                dve.drain()
                V.tensor_copy(best_f[:, :, :], best_at[:, :, 0:2])
                dve.drain()
                V.tensor_tensor(chosen[:, :, :, :], expert_no[:, :, :, :], best_f[:, :, :].unsqueeze(3).to_broadcast([P, TB, 2, E]), ALU.is_equal)
                dve.drain()
                V.tensor_tensor(mask[:, :, :], chosen[:, :, 0, :], chosen[:, :, 1, :], ALU.add)
                V.tensor_reduce(mask_sum[:, :], chosen[:, :, :, :].rearrange("p i k e -> p e (i k)"), AX.X, ALU.add)
                dve.drain()
                V.tensor_tensor(before[:, b + 1, :], before[:, b, :], mask_sum[:, :], ALU.add).then_inc(mask_set, 1)
                last_one = b == B - 1
                if last_one:
                    dve.wait_ge(total_mm, 1)
                    V.memset(blk_1[:, :], 1.0)
                    V.tensor_tensor(table_f[:, 4 * E:5 * E], total_ps, region_row[:, 0, :], ALU.add)
                    V.tensor_scalar(blk_f[:, :], total_ps, float(P - 1), None, ALU.add)
                dve.wait_ge(share_set, b + 1)
                V.tensor_scalar(share[:, :, :], share[:, :, :], tanh_f, None, ALU.mult)
                dve.drain()
                V.tensor_tensor(weighed[:, :, :, :], chosen[:, :, :, :], share[:, :, :].unsqueeze(3).to_broadcast([P, TB, 2, E]), ALU.mult)
                if last_one:
                    V.tensor_copy(blk_i[:, :], blk_f[:, :])
                dve.drain()
                V.tensor_tensor(rows[b][:, :, META:META + E], weighed[:, :, 0, :], weighed[:, :, 1, :], ALU.add)
                V.tensor_copy(rows[b][:, :, ROW - 1].bitcast(I32), token_no[:, b * TB:(b + 1) * TB])
                if last_one:
                    V.tensor_single_scalar(blk_j[:, :], blk_i[:, :], 7, ALU.logical_shift_right)
                dve.wait_ge(rank_mm, b + 1)
                V.tensor_tensor(place[:, :, :], rank_ps, region_row[:, :, :], ALU.add)
                dve.drain()
                V.tensor_tensor(place_of[:, :, :, :], chosen[:, :, :, :], place[:, :, :].unsqueeze(2).to_broadcast([P, TB, 2, E]), ALU.mult)
                if last_one:
                    V.tensor_copy(blk_f[:, :], blk_j[:, :])
                dve.drain()
                V.tensor_reduce(place_f[:, :, :], place_of[:, :, :, :], AX.X, ALU.add)
                if last_one:
                    V.tensor_scalar(table_f[:, 3 * E:4 * E], blk_f[:, :], 1.0, None, ALU.max)
                dve.drain()
                V.tensor_copy(place_i[:, b, :, :], place_f[:, :, :]).then_inc(place_set, 1)
                if last_one:
                    V.tensor_tensor_scan(table_f[:, E:2 * E], blk_1[:, :], table_f[:, 3 * E:4 * E], 0.0, ALU.mult, ALU.add)
                    dve.drain()
                    V.tensor_tensor(table_f[:, 0:E], table_f[:, E:2 * E], table_f[:, 3 * E:4 * E], ALU.subtract)
                    V.tensor_scalar(table_f[:, 2 * E:3 * E - 1], table_f[:, E:2 * E - 1], -1.0, None, ALU.add)
                    V.memset(table_f[:, 3 * E - 1:3 * E], float(1 << 16))
                    dve.drain()
                    V.tensor_copy(table[0:1, :], table_f[0:1, :]).then_inc(table_set, 1)
                if b == SOON - 1:
                    V.tensor_copy(early_i[:, :], early_ps)
                    dve.drain()
                    V.tensor_single_scalar(early_blocks[:, :], early_i[:, :], 7, ALU.logical_shift_right).then_inc(early_set, 1)

            def split_low(q, n, steps):
                for j in steps:
                    dve.wait_ge(hi_set[q], (n - 1) * OPS + j + 1)
                    V.tensor_tensor(w_lo[q][:, j, :], raw[:, q, j * OPW:(j + 1) * OPW], w_hi[q][:, j, :].bitcast(F32),
                                    ALU.subtract).then_inc(lo_set[q], 1)

            mask_A(0)
            mask_A(1)
            x_stats(2)
            x1(0)
            mask_A(2)
            x1(1)
            choose(0)
            x_stats(3)
            mask_A(3)
            for b in range(2, B):
                x1(b)
                choose(b - 1)
            choose(B - 1)

            V.memset(small[:, 5:6], 0.0).then_inc(y_out, 1)

            def x_low(n):
                dve.wait_ge(xhi_set, n)
                V.tensor_copy(meta_next[:, :], xtile[:, META:META + E])
                V.tensor_copy(token_next[:, :], xtile[:, ROW - 1:ROW].bitcast(I32)).then_inc(xtile_free, 1)
                V.tensor_tensor(xT_lo[:, :, :], bank[X_BANK][:, :].rearrange("p (c n) -> p c n", c=DC), xT_hi[:, :, :].bitcast(F32),
                                ALU.subtract).then_inc(xT_set, 1)

            def take_meta():
                dve.drain()
                V.tensor_copy(meta_now[:, :], meta_next[:, :])
                V.tensor_copy(token_now[:, :], token_next[:, :])
                dve.drain()

            def product(s, nth):
                dve.wait_ge(silu_set[s], nth)
                dve.wait_ge(up_mm[s], nth)
                V.tensor_tensor(h[:, s, :], bank[UP[s]][:, :], act_g[:, s, :], ALU.mult).then_inc(h_set[s], 1)

            def h_low(s, nth):
                dve.wait_ge(hhi_set[s], nth)
                V.tensor_tensor(hT_lo[:, s, :], bank[H_BANK[s]][:, :], hT_hi[:, s, :].bitcast(F32), ALU.subtract).then_inc(hT_set[s], 1)

            x_low(1)
            take_meta()
            split_low(2, 1, range(OPS))
            with dve.Fori(0, E) as e:
                change = entry(dve, 2, e, 0, 1 << 20)
                after = dve.snap(e + 2)
                with blocks(dve, e) as g:
                    nth = dve.snap(g + 1)
                    product(0, nth)
                    h_low(0, nth)
                    product(1, nth)
                    x_low(nth + 1)
                    h_low(1, nth)
                    with dve.If(g == change):
                        split_low(0, after, range(3))
                    with dve.Else():
                        dve.nop()
                    dve.wait_ge(y_mm, nth)
                    dve.wait_ge(y_added, g * 16 + 16)
                    V.tensor_scalar(y[:, :], bank[Y_BANK][:, :], meta_now[:, bass.ds(e, 1)], None, ALU.mult).then_inc(y_out, 1)
                    V.tensor_copy(token_out[:, :], token_now[:, :]).then_inc(y_set, 1)
                    take_meta()
                    with dve.If(g == change):
                        split_low(0, after, range(3, OPS))
                        split_low(1, after, range(OPS))
                    with dve.Else():
                        dve.nop()
                    dve.nop()


def kernel(x, ctx_512, g_xattn, g_ffn, L0_xattn_Wq, L0_xattn_Wk, L0_xattn_gamma_raw, L0_ffn_gate_w,
           L0_ffn_w1, L0_ffn_w2, L0_ffn_w3):
    import numpy as np
    import concourse.bacc as bacc
    from concourse.bass_utils import run_bass_kernel_spmd

    def plain(a):
        return np.ascontiguousarray(np.asarray(a))

    w1, w2, w3 = (plain(a) for a in (L0_ffn_w1, L0_ffn_w2, L0_ffn_w3))
    first = np.stack([w1, w3], axis=0).reshape(2, E, 2, COLS, DC, P).transpose(1, 5, 2, 4, 0, 3)
    second = w2.reshape(E, D, IC, P).transpose(0, 3, 2, 1)
    arrays = {
        "x": plain(x).reshape(TOKENS, D),
        "ctxT": plain(plain(ctx_512).transpose(2, 0, 1)),
        "wqT": plain(plain(L0_xattn_Wq).T),
        "wkT": plain(plain(L0_xattn_Wk).T),
        "gateT": plain(plain(L0_ffn_gate_w).T.reshape(DC, P, E).transpose(1, 0, 2)),
        "weights": plain(np.concatenate([first.reshape(E, P, -1), second.reshape(E, P, -1)], axis=2)),
        "gains": plain(np.concatenate([plain(a).reshape(-1) for a in (g_xattn, L0_xattn_gamma_raw, g_ffn)])),
    }
    nc = bacc.Bacc("TRN2", target_bir_lowering=False, num_devices=1)
    aps = [nc.dram_tensor(k, a.shape, mybir.dt.from_np(a.dtype), kind="ExternalInput").ap() for k, a in arrays.items()]
    out = nc.dram_tensor("out", (TOKENS + P, D), F32, kind="ExternalOutput").ap()
    build(nc, *aps, out)
    result = run_bass_kernel_spmd(nc, [arrays], core_ids=[0])
    return result.results[0]["out"][0:TOKENS].reshape(B, N, D)
```
